# Optimizing a Trainium2 kernel written in Bass

```python
import numpy as np
import jax
import jax.numpy as jnp

def _softmax(x, axis=-1):
    return jax.nn.softmax(x, axis=axis)

def _gelu(x):
    return jax.nn.gelu(x, approximate=True)

def _silu(x):
    return jax.nn.silu(x)

def _sigmoid(x):
    return jax.nn.sigmoid(x)

def _layernorm(x, axis=-1, eps=1e-05):
    m = jnp.mean(x, axis=axis, keepdims=True)
    v = jnp.var(x, axis=axis, keepdims=True)
    return (x - m) / jnp.sqrt(v + eps)

def _scatter_add(tgt, idx, src, axis=0):
    return tgt.at[idx].add(src)

def _segment_sum(src, seg, n):
    return jax.ops.segment_sum(src, seg, n)
kernel_name = 'mk_macaron_d1_jaxref_r4_9a4957'

def setup_inputs(seed: int=0):
    np.random.seed(seed)
    _w = jnp.asarray

    def _L0_attn_setup():
        import jax, jax.numpy as jnp
        import numpy as np
        D_MODEL = 256
        D_STATE = 16
        D_CONV = 4
        EXPAND = 2
        HEADDIM = 8
        D_INNER = EXPAND * D_MODEL
        NHEADS = D_INNER // HEADDIM
        CONV_DIM = D_INNER + 2 * D_STATE
        D_IN_PROJ = 2 * D_INNER + 2 * D_STATE + NHEADS
        B_SZ, SEQ = (4, 512)
        EPS = 1e-05

        def _mamba_block(x, ln_w, ln_b, W_in, conv_w, conv_b, A_log, Dp, dt_bias, rms_w, W_out):
            B, L, _ = x.shape
            mu = jnp.mean(x, axis=-1, keepdims=True)
            var = jnp.mean((x - mu) ** 2, axis=-1, keepdims=True)
            xn = (x - mu) * jax.lax.rsqrt(var + EPS) * ln_w + ln_b
            u = xn @ W_in
            z = u[..., :D_INNER]
            xBC = u[..., D_INNER:D_INNER + CONV_DIM]
            dt = jax.nn.softplus(u[..., -NHEADS:] + dt_bias)
            xp = jnp.pad(xBC, ((0, 0), (D_CONV - 1, 0), (0, 0)))
            xBC = jax.lax.conv_general_dilated(xp, conv_w, window_strides=(1,), padding='VALID', dimension_numbers=('NWC', 'WIO', 'NWC'), feature_group_count=CONV_DIM)
            xBC = jax.nn.silu(xBC + conv_b)
            xs = xBC[..., :D_INNER].reshape(B, L, NHEADS, HEADDIM)
            Bm = xBC[..., D_INNER:D_INNER + D_STATE]
            Cm = xBC[..., D_INNER + D_STATE:]
            A = -jnp.exp(A_log)

            def step(h, inp):
                x_t, B_t, C_t, dt_t = inp
                dA = jnp.exp(dt_t * A)
                h = h * dA[..., None, None] + jnp.einsum('bh,bhp,bn->bhpn', dt_t, x_t, B_t)
                y = jnp.einsum('bhpn,bn->bhp', h, C_t)
                return (h, y)
            h0 = jnp.zeros((B, NHEADS, HEADDIM, D_STATE), x.dtype)
            _, ys = jax.lax.scan(step, h0, (xs.swapaxes(0, 1), Bm.swapaxes(0, 1), Cm.swapaxes(0, 1), dt.swapaxes(0, 1)))
            y = ys.swapaxes(0, 1) + Dp[None, None, :, None] * xs
            y = y.reshape(B, L, D_INNER)
            g = y * jax.nn.silu(z)
            g = g * jax.lax.rsqrt(jnp.mean(g * g, axis=-1, keepdims=True) + EPS) * rms_w
            return x + g @ W_out
        key = jax.random.key(seed)
        ks = jax.random.split(key, 8)
        return {'x': jax.random.normal(ks[0], (B_SZ, SEQ, D_MODEL), jnp.float32), 'ln_w': jnp.ones((D_MODEL,), jnp.float32), 'ln_b': jnp.zeros((D_MODEL,), jnp.float32), 'W_in': jax.random.normal(ks[1], (D_MODEL, D_IN_PROJ), jnp.float32) * 0.02, 'conv_w': jax.random.normal(ks[2], (D_CONV, 1, CONV_DIM), jnp.float32) * 0.2, 'conv_b': jnp.zeros((CONV_DIM,), jnp.float32), 'A_log': jnp.log(jax.random.uniform(ks[3], (NHEADS,), jnp.float32, 1.0, 16.0)), 'Dp': jnp.ones((NHEADS,), jnp.float32) + 0.1 * jax.random.normal(ks[4], (NHEADS,), jnp.float32), 'dt_bias': 0.5 * jax.random.normal(ks[5], (NHEADS,), jnp.float32), 'rms_w': jnp.ones((D_INNER,), jnp.float32), 'W_out': jax.random.normal(ks[6], (D_INNER, D_MODEL), jnp.float32) * 0.02}
    _L0_attn_in = _L0_attn_setup()

    def _L0_ffn_setup():
        import jax, jax.numpy as jnp
        import numpy as np
        B, T, D, E, H, K = (4, 512, 256, 8, 512, 2)
        key = jax.random.key(seed)
        k0, k1, k2, k3 = jax.random.split(key, 4)
        x = jax.random.normal(k0, (B, T, D), dtype=jnp.float32)
        router_w = jax.random.normal(k1, (E, D), dtype=jnp.float32) * D ** (-0.5)
        w1 = jax.random.normal(k2, (E, D, H), dtype=jnp.float32) * D ** (-0.5)
        w2 = jax.random.normal(k3, (E, H, D), dtype=jnp.float32) * H ** (-0.5)
        return {'x': x, 'router_w': router_w, 'w1': w1, 'w2': w2}
    _L0_ffn_in = _L0_ffn_setup()
    _d = {'L0_attn_x': _L0_attn_in['x'], 'L0_attn_ln_w': _L0_attn_in['ln_w'], 'L0_attn_ln_b': _L0_attn_in['ln_b'], 'L0_attn_W_in': _L0_attn_in['W_in'], 'L0_attn_conv_w': _L0_attn_in['conv_w'], 'L0_attn_conv_b': _L0_attn_in['conv_b'], 'L0_attn_A_log': _L0_attn_in['A_log'], 'L0_attn_Dp': _L0_attn_in['Dp'], 'L0_attn_dt_bias': _L0_attn_in['dt_bias'], 'L0_attn_rms_w': _L0_attn_in['rms_w'], 'L0_attn_W_out': _L0_attn_in['W_out'], 'L0_ffn_router_w': _L0_ffn_in['router_w'], 'L0_ffn_w1': _L0_ffn_in['w1'], 'L0_ffn_w2': _L0_ffn_in['w2']}
    _x0 = _d['L0_attn_x']
    _d['L0_attn_x'] = jax.random.normal(jax.random.fold_in(jax.random.key(seed), 1), (4, 1024, 256), dtype=_x0.dtype)
    del _x0
    return _d

def reference(L0_attn_x, L0_attn_ln_w, L0_attn_ln_b, L0_attn_W_in, L0_attn_conv_w, L0_attn_conv_b, L0_attn_A_log, L0_attn_Dp, L0_attn_dt_bias, L0_attn_rms_w, L0_attn_W_out, L0_ffn_router_w, L0_ffn_w1, L0_ffn_w2):

    def _L0_attn_ref(x, ln_w, ln_b, W_in, conv_w, conv_b, A_log, Dp, dt_bias, rms_w, W_out):
        import jax, jax.numpy as jnp
        import numpy as np
        D_MODEL = 256
        D_STATE = 16
        D_CONV = 4
        EXPAND = 2
        HEADDIM = 8
        D_INNER = EXPAND * D_MODEL
        NHEADS = D_INNER // HEADDIM
        CONV_DIM = D_INNER + 2 * D_STATE
        D_IN_PROJ = 2 * D_INNER + 2 * D_STATE + NHEADS
        B_SZ, SEQ = (4, 512)
        EPS = 1e-05

        def _mamba_block(x, ln_w, ln_b, W_in, conv_w, conv_b, A_log, Dp, dt_bias, rms_w, W_out):
            B, L, _ = x.shape
            mu = jnp.mean(x, axis=-1, keepdims=True)
            var = jnp.mean((x - mu) ** 2, axis=-1, keepdims=True)
            xn = (x - mu) * jax.lax.rsqrt(var + EPS) * ln_w + ln_b
            u = xn @ W_in
            z = u[..., :D_INNER]
            xBC = u[..., D_INNER:D_INNER + CONV_DIM]
            dt = jax.nn.softplus(u[..., -NHEADS:] + dt_bias)
            xp = jnp.pad(xBC, ((0, 0), (D_CONV - 1, 0), (0, 0)))
            xBC = jax.lax.conv_general_dilated(xp, conv_w, window_strides=(1,), padding='VALID', dimension_numbers=('NWC', 'WIO', 'NWC'), feature_group_count=CONV_DIM)
            xBC = jax.nn.silu(xBC + conv_b)
            xs = xBC[..., :D_INNER].reshape(B, L, NHEADS, HEADDIM)
            Bm = xBC[..., D_INNER:D_INNER + D_STATE]
            Cm = xBC[..., D_INNER + D_STATE:]
            A = -jnp.exp(A_log)

            def step(h, inp):
                x_t, B_t, C_t, dt_t = inp
                dA = jnp.exp(dt_t * A)
                h = h * dA[..., None, None] + jnp.einsum('bh,bhp,bn->bhpn', dt_t, x_t, B_t)
                y = jnp.einsum('bhpn,bn->bhp', h, C_t)
                return (h, y)
            h0 = jnp.zeros((B, NHEADS, HEADDIM, D_STATE), x.dtype)
            _, ys = jax.lax.scan(step, h0, (xs.swapaxes(0, 1), Bm.swapaxes(0, 1), Cm.swapaxes(0, 1), dt.swapaxes(0, 1)))
            y = ys.swapaxes(0, 1) + Dp[None, None, :, None] * xs
            y = y.reshape(B, L, D_INNER)
            g = y * jax.nn.silu(z)
            g = g * jax.lax.rsqrt(jnp.mean(g * g, axis=-1, keepdims=True) + EPS) * rms_w
            return x + g @ W_out
        return _mamba_block(x, ln_w, ln_b, W_in, conv_w, conv_b, A_log, Dp, dt_bias, rms_w, W_out)

    def _L0_ffn_ref(x, router_w, w1, w2):
        import jax, jax.numpy as jnp
        import numpy as np
        B, T, D, E, H, K = (4, 512, 256, 8, 512, 2)
        Bb, Tt, Dd = x.shape
        N = Bb * Tt
        logits = jnp.einsum('btd,ed->bte', x, router_w)
        top_vals, top_idx = jax.lax.top_k(logits, K)
        top_w = jax.nn.softmax(top_vals, axis=-1)
        xf = x.reshape(N, Dd)
        h = jnp.einsum('nd,edh->enh', xf, w1)
        h = jnp.square(jax.nn.relu(h))
        y = jnp.einsum('enh,ehd->end', h, w2)
        idx_f = top_idx.reshape(N, K)
        w_f = top_w.reshape(N, K)
        y_sel = y[idx_f, jnp.arange(N)[:, None]]
        out = jnp.einsum('nk,nkd->nd', w_f, y_sel)
        return out.reshape(Bb, Tt, Dd)
    x = L0_attn_x
    x = x + 0.5 * _L0_ffn_ref(_layernorm(x, axis=-1), L0_ffn_router_w, L0_ffn_w1, L0_ffn_w2)
    x = x + _L0_attn_ref(_layernorm(x, axis=-1), L0_attn_ln_w, L0_attn_ln_b, L0_attn_W_in, L0_attn_conv_w, L0_attn_conv_b, L0_attn_A_log, L0_attn_Dp, L0_attn_dt_bias, L0_attn_rms_w, L0_attn_W_out)
    x = x + 0.5 * _L0_ffn_ref(_layernorm(x, axis=-1), L0_ffn_router_w, L0_ffn_w1, L0_ffn_w2)
    return x

_drawn_inputs = setup_inputs


def setup_inputs(seed=0):
    import zlib

    import numpy as np

    out = dict(_drawn_inputs(seed))
    spreads = {'L0_attn_ln_w': (1.0, 0.2),
     'L0_attn_ln_b': (0.0, 0.1),
     'L0_attn_conv_b': (0.0, 0.1),
     'L0_attn_rms_w': (1.0, 0.2)}
    factors = {'L0_attn_A_log': 64.0, 'L0_attn_dt_bias': 8.0}
    for name, (base, spread) in spreads.items():
        noise = np.random.default_rng([zlib.crc32(name.encode()), seed]).standard_normal(out[name].shape)
        drawn = base * np.exp(spread * noise) if base else spread * noise
        out[name] = jnp.asarray(drawn.astype(out[name].dtype))
    for name, factor in factors.items():
        out[name] = (out[name] * factor).astype(out[name].dtype)
    return out
```

```python
import math
from contextlib import ExitStack

import concourse.bass as bass
from concourse import mybir

F32, F16 = mybir.dt.float32, mybir.dt.float16
U32, I32 = mybir.dt.uint32, mybir.dt.int32
ALU = mybir.AluOpType
ACT = mybir.ActivationFunctionType
AX = mybir.AxisListType
ds = bass.ds

P = 128
B, T, D = 4, 1024, 256
E, HID = 8, 512
QT = P // B
NT = B * T // P
KD, KH = D // P, HID // P
CAP = B * T + P
NS = 2 * NT + E
WSCALE = 64.0
EPS = 1e-5
DI, DS_, DC, NH = 512, 16, 4, 64
HP = DI // NH
NB = DI // P

C_ID, C_INC, C_GT, C_BLK, C_HALF, C_QM, C_BM, C_IOTA, C_ECAP, C_TRI, C_TAB = range(11)
STAGE = 2
ARENA = 8 * 1024
CLAMP = -110.0
DOWN = 2.0 ** -20
A_LOG_MAX = 88.0
C_W = [P, P, P, B * DS_, P, QT, B, E, E, 1, NS]
C_OFF = [sum(C_W[:i]) for i in range(len(C_W) + 1)]


V_LNW, V_LNB, V_CW, V_CB, V_RMS, V_DTB, V_DP, V_AL = range(8)
V_W = [KD, KD, (NB + 1) * DC, NB + 1, NB, NH, NH, NH]
V_OFF = [sum(V_W[:i]) for i in range(len(V_W) + 1)]


RUN = dict.fromkeys(("var", "rstd", "count_ps", "pad", "table", "slots"), 1)
RUN |= dict.fromkeys(("xh", "xh_free", "hi", "lo", "logit_ps", "dm", "ohb", "rank_ps", "scat_free", "ed", "xt_ps", "xt",
                      "slot", "drow_free", "yg_free", "gi"), NT)
RUN |= dict.fromkeys(("turned", "xin_free", "xth", "xth_free", "up", "h_free", "hr", "hq", "hh", "hh_free", "hl", "hl_free",
                      "down", "y_free", "ysb"), NS)
RUN |= {"ohacc": NT + 1, "padded": 16 * E, "scat": 16 * NT, "xin": 8 * NS, "yst": 8 * NS, "yg": 16 * NT, "xnew": 0}
TABLE_STEPS = 43


class Chain:

    def __init__(self, eng, sem, per_tile, before=0):
        self.eng, self.sem, self.per, self.before = eng, sem, per_tile, before

    def at(self, tile):
        self.base, self.n = tile * self.per + self.before * self.per, 0

    def link(self, ins):
        self.n += 1
        ins.then_inc(self.sem, 1)
        self.eng.wait_ge(self.sem, self.base + self.n)

    def done(self):
        assert self.n == self.per, (self.n, self.per)


def build(nc, a, out):
    with ExitStack() as ctx:
        def sb(name, shape, dt=F32):
            return ctx.enter_context(nc.sbuf_tensor(name, shape, dt))

        def sem(name):
            return ctx.enter_context(nc.semaphore(name))

        banks = [ctx.enter_context(nc.psum_tensor(f"bank{i}", [P, 512], F32)) for i in range(8)]

        X = sb("X", [P, NT * D])
        w1 = {h: sb(f"w1{h}", [P, E * KD * HID], F16) for h in "hl"}
        w2 = {h: sb(f"w2{h}", [P, E * KH * D], F16) for h in "hl"}
        rw = sb("rw", [P, KD * E])
        cst = sb("cst", [P, C_OFF[-1]])
        cst16 = sb("cst16", [P, 3 * P], F16)

        def const(i, n=None):
            return cst[:, C_OFF[i]:C_OFF[i] + (n or C_W[i])]

        ident = const(C_ID)
        ident16, before16, ones16 = (cst16[:, i * P:(i + 1) * P] for i in range(3))
        mv = sb("mv", [P, 2 * NT])
        var = sb("var", [P, NT])
        rstd = sb("rstd", [P, NT])
        mhalf = sb("mhalf", [P, NT])

        disp = nc.dram_tensor("disp", (E * CAP, 2 * D), F16, kind="Internal").ap()
        yrows = nc.dram_tensor("yrows", (NS * P, D), F32, kind="Internal").ap()

        arena = sb("arena", [P, ARENA])
        used = [0]

        def carve(cols, dt=F32, rows=P):
            n = cols * (1 if dt != F16 else 0) or cols // 2
            at, used[0] = used[0], used[0] + n
            assert used[0] <= ARENA, used[0]
            v = arena[0:rows, at:at + n]
            return v if dt == F32 else v.bitcast(dt)

        xh = [carve(D) for p in range(2)]
        drow = [carve(2 * D, F16) for p in range(2)]
        xT = [carve(D) for p in range(2)]
        lg = [sb(f"lg{p}", [P, E]) for p in range(2)]
        mx = [sb(f"mx{p}", [P, E]) for p in range(2)]
        ix = [sb(f"ix{p}", [P, E], U32) for p in range(2)]
        ixf = [sb(f"ixf{p}", [P, 2]) for p in range(2)]
        oh = [sb(f"oh{p}", [P, 2 * E]) for p in range(2)]
        ohb = [sb(f"ohb{p}", [P, E], F16) for p in range(2)]
        ohacc = [sb(f"ohacc{p}", [P, E], F16) for p in range(2)]
        dm = [sb(f"dm{p}", [P, 1]) for p in range(2)]
        ed = [sb(f"ed{p}", [P, 1]) for p in range(2)]
        den = [sb(f"den{p}", [P, 2]) for p in range(2)]
        rk = [sb(f"rk{p}", [P, E]) for p in range(2)]
        junk = sb("junk", [P, 2 * E])
        slotf = [sb(f"slotf{p}", [P, 2]) for p in range(2)]
        sloti = [sb(f"sloti{p}", [P, 2], U32) for p in range(2)]
        slots = sb("slots", [P, 2 * NT], U32)
        slotd = sb("slotd", [P, 2 * NT])
        eidx = sb("eidx", [P, 2 * NT])
        eadd = sb("eadd", [P, 2 * NT])
        shift = sb("shift", [P, E])
        wts = sb("wts", [P, 2 * NT])
        zrow = sb("zrow", [P, 2 * D], F16)
        cnt = sb("cnt", [P, E])
        pade = sb("pade", [P, E])
        padi = sb("padi", [P, E], U32)
        nti = sb("nti", [P, E], I32)
        ntf = sb("ntf", [P, 2 * E])
        cum = sb("cum", [P, E])
        skip = sb("skip", [P, E])
        tcl = sb("tcl", [1, NS])
        past = sb("past", [1, NS * E])
        tabf = sb("tabf", [1, 2 * NS])
        tabi = sb("tabi", [1, 2 * NS], I32)
        route_end = used[0]
        xin = [carve(2 * D, F16) for p in range(2)]
        xTh = [carve(4 * P, F16) for p in range(2)]
        hr = [carve(HID) for p in range(2)]
        hq = [carve(HID) for p in range(2)]
        hh = [carve(HID, F16) for p in range(2)]
        hl = [carve(HID, F16) for p in range(2)]
        ysb = [carve(D) for p in range(2)]
        used[0] = route_end
        stage = [carve(2048) for p in range(2)]
        gi = [sb(f"gi{p}", [P, 2], U32) for p in range(2)]
        yg = [[sb(f"yg{p}{j}", [P, D]) for j in range(2)] for p in range(2)]
        mv1 = [sb(f"mv1{p}", [P, 2]) for p in range(2)]
        st = [sb(f"st{p}", [P, 6]) for p in range(2)]

        used[0] = 0
        R = [carve(NH * QT) for p in range(2)]
        bd = [carve(NH * B * HP) for p in range(2)]
        wz = sb("wz", [P, KD * DI])
        wx = sb("wx", [P, KD * DI])
        wbc = sb("wbc", [P, KD * P])
        wdt = sb("wdt", [P, KD * NH])
        wo = sb("wo", [P, NB * D])
        vec = sb("vec", [P, V_OFF[-1]])
        negA = sb("negA", [P, NH])
        xm = sb("xm", [P, D])
        xn = sb("xn", [P, D])
        xnT = [sb(f"xnT{p}", [P, D]) for p in range(2)]
        U = [sb(f"U{p}", [P, (NB + 1) * B * (QT + DC - 1)]) for p in range(2)]
        cv = sb("cv", [P, (NB + 1) * P])
        th = sb("th", [P, (NB + 1) * P])
        bm = sb("bm", [B * DS_, P])
        cm = [sb(f"cm{p}", [B * DS_, P]) for p in range(2)]
        bt = [sb(f"bt{p}", [P, B * DS_]) for p in range(2)]
        cbr = sb("cbr", [P, QT])
        cb = [sb(f"cb{p}", [P, QT]) for p in range(2)]
        xs = [sb(f"xs{p}", [P, DI]) for p in range(2)]
        dtx = [sb(f"dtx{p}", [P, DI]) for p in range(2)]
        dv = sb("dv", [P, 8 * NH])
        dt_ = [sb(f"dt{p}", [P, NH]) for p in range(2)]
        a_ = [sb(f"a{p}", [P, NH]) for p in range(2)]
        ee = sb("ee", [P, 2 * NH])
        dd = sb("dd", [B * DS_, NH])
        Hs = sb("Hs", [B * DS_, DI])
        dtxw = sb("dtxw", [P, DI])
        yi = sb("yi", [P, DI])
        y1 = sb("y1", [P, DI])
        y2 = sb("y2", [P, DI])
        xd = sb("xd", [P, DI])
        tz = sb("tz", [P, DI])
        gz = sb("gz", [P, DI])
        G = sb("G", [P, DI])
        GT = yi
        ma = sb("ma", [P, 6 + 2 + 2])
        mb = sb("mb", [P, 6 + 2 + 2])
        mss = sb("mss", [P, 3])

        s = {}

        def S(name):
            if name not in s:
                s[name] = sem(name)
            return s[name]

        def hold(eng, name):
            eng.sem_inc(S(f"held_{name}"), 1)

        def Xk(k):
            return X[:, ds(k * D, D)] if not isinstance(k, int) else X[:, k * D:(k + 1) * D]

        def row(t, k, n):
            return t[:, ds(k * n, n)]

        xv = a["x"].rearrange("b (k t) d -> k b t d", t=QT)
        ov = out.rearrange("b (k t) d -> k b t d", t=QT)
        NCHUNK = E * KD * HID // 2048

        def sync_load(sp):
            sp.dma_start(cst[:, :], a["consts"]).then_inc(S("const_in"), 16)
            sp.dma_start(cst16[:, :], a["consts16"]).then_inc(S("const_in"), 16)
            sp.dma_start(rw[:, :], a["router"].rearrange("(c p) e -> p c e", p=P)).then_inc(S("const_in"), 16)
            for b in range(B):
                sp.dma_start(X[b * QT:(b + 1) * QT, :].rearrange("t (k d) -> t k d", d=D),
                             a["x"][b].rearrange("(k t) d -> t k d", t=QT)).then_inc(S("x_in"), 16)
            views = ([a["w1"][e].rearrange("(c p) h -> p c h", p=P) for e in range(E)],
                     [a["w2"][e].rearrange("(c p) d -> p c d", p=P) for e in range(E)])
            n = 0
            for v in views:
                for c in range(NCHUNK):
                    if n >= 2:
                        sp.wait_ge(S("stage_used"), n - 1)
                    for j in range(2):
                        sp.dma_start(stage[n % 2][:, j * 1024:(j + 1) * 1024].rearrange("p (c h) -> p c h", c=v[0].shape[1]),
                                     v[2 * c + j]).then_inc(S(f"stage_in{n % 2}"), 16)
                    n += 1

        def split_weights(dve, act):
            n = 0
            for w in (w1, w2):
                for c in range(NCHUNK):
                    hi, lo = (w[h][:, c * 2048:(c + 1) * 2048] for h in "hl")
                    if act:
                        act.wait_ge(S(f"stage_in{n % 2}"), 32 * (n // 2 + 1))
                        act.activation(hi, stage[n % 2][:, :], ACT.Copy, scale=WSCALE).then_inc(S("high_done"), 1)
                    else:
                        dve.wait_ge(S("high_done"), n + 1)
                        dve.scalar_tensor_tensor(out=lo, in0=stage[n % 2][:, :], scalar=WSCALE, in1=hi,
                                                 op0=ALU.mult, op1=ALU.subtract).then_inc(S("stage_used"), 1)
                    n += 1

        def stats(dve, r):
            ch = Chain(dve, S("stats_chain"), 3, r * NT)
            with dve.Fori(0, NT // 2) as i:
                for p in range(2):
                    k = i * 2 + p
                    ch.at(k)
                    ch.link(dve.bn_stats(st[p][:, :], Xk(k)))
                    hold(dve, "dve")
                    ch.link(dve.bn_aggr(mv1[p][:, :], st[p][:, :]))
                    ch.link(dve.tensor_copy(row(mv, k, 2), mv1[p][:, :]))
                    ch.done()
            v = mv[:, :].rearrange("p (k two) -> p k two", two=2)[:, :, 1]
            dve.tensor_scalar(var[:, :], v, EPS, None, ALU.add).then_inc(S("var"), 1)

        def pool_rstd(pool, r):
            if r == 0:
                pool.memset(mhalf[:, :], -0.5).then_inc(S("mhalf_set"), 1)
                pool.memset(zrow[:, :], 0.0).then_inc(S("zrow_set"), 1)
            pool.wait_ge(S("mhalf_set"), 1)
            pool.wait_ge(S("var"), 1 + r * RUN["var"])
            pool.tensor_tensor(rstd[:, :], var[:, :], mhalf[:, :], ALU.pow).then_inc(S("rstd"), 1)

        def route_dve(dve, r):
            ch = Chain(dve, S("route_chain"), 14, r * NT)
            dve.wait_ge(S("rstd"), 1 + r * RUN["rstd"])
            dve.memset(ohacc[0][:, :], 0.0).then_inc(S("ohacc"), 1)
            dve.wait_ge(S("const_in"), 48)
            if r == 0:
                dve.sem_inc(S("xh_free"), 2)
            with dve.Fori(0, NT // 2) as i:
                for p in range(2):
                    k = i * 2 + p
                    ch.at(k)
                    dve.wait_ge(S("xh_free"), k + 1 + r * RUN["xh_free"])
                    dve.tensor_scalar(xh[p][:, :], Xk(k), row(mv, k, 2)[:, 0:1], row(rstd, k, 1),
                                      ALU.subtract, ALU.mult).then_inc(S("xh"), 1)
                    dve.wait_ge(S("hi"), k + 1 + r * RUN["hi"])
                    dve.tensor_tensor(drow[p][:, D:2 * D], xh[p][:, :], drow[p][:, 0:D], ALU.subtract)\
                        .then_inc(S("lo"), 1)
                    dve.wait_ge(S("logit_ps"), k + 1 + r * RUN["logit_ps"])
                    ch.link(dve.tensor_copy(lg[p][:, :], banks[2 + p][:, 0:E]))
                    hold(dve, "dve")
                    ch.link(dve.max(out=mx[p][:, :], in_=lg[p][:, :]))
                    dve.tensor_tensor(dm[p][:, :], mx[p][:, 1:2], mx[p][:, 0:1], ALU.subtract).then_inc(S("dm"), 1)
                    hold(dve, "dve")
                    ch.link(dve.max_index(ix[p][:, :], mx[p][:, :], lg[p][:, :]))
                    ch.link(dve.tensor_copy(ixf[p][:, :], ix[p][:, 0:2]))
                    for j in range(2):
                        ch.link(dve.tensor_scalar(oh[p][:, j * E:(j + 1) * E], const(C_IOTA), ixf[p][:, j:j + 1], None,
                                                  ALU.is_equal))
                    dve.tensor_tensor(ohb[p][:, :], oh[p][:, 0:E], oh[p][:, E:2 * E], ALU.add).then_inc(S("ohb"), 1)
                    dve.wait_ge(S("ohb"), k + 1 + r * RUN["ohb"])
                    dve.wait_ge(S("ohacc"), k + 1 + r * RUN["ohacc"])
                    dve.wait_ge(S("rank_ps"), k + 1 + r * RUN["rank_ps"])
                    dve.tensor_tensor(ohacc[1 - p][:, :], ohacc[p][:, :], ohb[p][:, :], ALU.add)\
                        .then_inc(S("ohacc"), 1)
                    ch.link(dve.tensor_tensor(rk[p][:, :], banks[4 + p][:, 0:E], const(C_ECAP), ALU.add))
                    ch.link(dve.tensor_tensor_reduce(junk[:, 0:E], rk[p][:, :], oh[p][:, 0:E], 1.0, 0.0, ALU.mult,
                                                     ALU.add, slotf[p][:, 0:1]))
                    ch.link(dve.tensor_tensor_reduce(junk[:, E:2 * E], rk[p][:, :], oh[p][:, E:2 * E], 1.0, 0.0,
                                                     ALU.mult, ALU.add, slotf[p][:, 1:2]))
                    dve.wait_ge(S("scat_free"), k + 1 + r * RUN["scat_free"])
                    ch.link(dve.tensor_copy(row(slotd, k, 2), slotf[p][:, :]))
                    ch.link(dve.tensor_copy(row(eidx, k, 2), ixf[p][:, :]))
                    dve.tensor_copy(sloti[p][:, :], slotf[p][:, :]).then_inc(S("slot"), 1)
                    dve.wait_ge(S("ed"), k + 1 + r * RUN["ed"])
                    ch.link(dve.tensor_scalar(den[p][:, 0:1], ed[p][:, :], 1.0, 2.0 * WSCALE, ALU.add, ALU.mult))
                    ch.link(dve.reciprocal(row(wts, k * 2, 1), den[p][:, 0:1]))
                    ch.link(dve.tensor_tensor(wts[:, ds(k * 2 + 1, 1)], row(wts, k * 2, 1), ed[p][:, :], ALU.mult))
                    ch.done()
            dve.wait_ge(S("count_ps"), 1 + r * RUN["count_ps"])
            c2 = Chain(dve, S("table_chain"), TABLE_STEPS, r)
            c2.at(0)
            c2.link(dve.tensor_copy(cnt[:, :], banks[4][:, 0:E]))
            c2.link(dve.tensor_tensor(pade[:, :], cnt[:, :], const(C_ECAP), ALU.add))
            c2.link(dve.tensor_scalar(pade[:, :], pade[:, :], const(C_TRI), None, ALU.add))
            c2.link(dve.tensor_copy(padi[:, :], pade[:, :]))
            dve.sem_inc(S("pad"), 1)
            c2.link(dve.tensor_scalar(ntf[:, 0:E], cnt[:, :], float(P - 1), None, ALU.add))
            c2.link(dve.tensor_copy(nti[:, :], ntf[:, 0:E]))
            c2.link(dve.tensor_scalar(nti[:, :], nti[:, :], int(math.log2(P)), None, ALU.arith_shift_right))
            c2.link(dve.tensor_copy(ntf[:, 0:E], nti[:, :]))
            c2.link(dve.tensor_copy(cum[:, 0:1], ntf[:, 0:1]))
            for e in range(1, E):
                c2.link(dve.tensor_tensor(cum[:, e:e + 1], cum[:, e - 1:e], ntf[:, e:e + 1], ALU.add))
            c2.link(dve.tensor_scalar(skip[:, :], ntf[:, 0:E], -float(P), float(CAP), ALU.mult, ALU.add))
            c2.link(dve.tensor_scalar(ntf[:, E:E + 1], cum[:, E - 1:E], -1.0, None, ALU.add))
            c2.link(dve.tensor_scalar(tcl[:, :], cst[0:1, C_OFF[C_TAB]:C_OFF[C_TAB] + NS], ntf[0:1, E:E + 1], None, ALU.min))
            pv = past[:, :].rearrange("o (t e) -> o t e", e=E)
            c2.link(dve.tensor_tensor(pv, tcl[:, :].unsqueeze(2).to_broadcast([1, NS, E]),
                                      cum[0:1, :].unsqueeze(1).to_broadcast([1, NS, E]), ALU.is_ge))
            c2.link(dve.tensor_reduce(tabf[:, 0:NS], pv, AX.X, ALU.add))
            c2.link(dve.tensor_tensor(pv, pv, skip[0:1, :].unsqueeze(1).to_broadcast([1, NS, E]), ALU.mult))
            c2.link(dve.tensor_reduce(tabf[:, NS:2 * NS], pv, AX.X, ALU.add))
            c2.link(dve.scalar_tensor_tensor(out=tabf[:, NS:2 * NS], in0=tcl[:, :], scalar=float(P),
                                             in1=tabf[:, NS:2 * NS], op0=ALU.mult, op1=ALU.add))
            c2.link(dve.tensor_copy(tabi[:, :], tabf[:, :]))
            dve.sem_inc(S("table"), 1)
            c2.link(dve.tensor_tensor(shift[:, :], cum[:, :], ntf[:, 0:E], ALU.subtract))
            c2.link(dve.scalar_tensor_tensor(out=shift[:, :], in0=shift[:, :], scalar=float(P), in1=const(C_ECAP),
                                             op0=ALU.mult, op1=ALU.subtract))
            for e in range(E):
                c2.link(dve.tensor_scalar(eadd[:, :], eidx[:, :], float(e), shift[:, e:e + 1], ALU.is_equal, ALU.mult))
                c2.link(dve.tensor_tensor(slotd[:, :], slotd[:, :], eadd[:, :], ALU.add))
            dve.tensor_copy(slots[:, :], slotd[:, :]).then_inc(S("slots"), 1)
            c2.done()

        def route_act(act, r):
            if r == 0:
                act.sem_inc(S("drow_free"), 2)
            with act.Fori(0, NT // 2) as i:
                for p in range(2):
                    k = i * 2 + p
                    act.wait_ge(S("xh"), k + 1 + r * RUN["xh"])
                    act.wait_ge(S("drow_free"), k + 1 + r * RUN["drow_free"])
                    act.activation(drow[p][:, 0:D], xh[p][:, :], ACT.Copy).then_inc(S("hi"), 1)
                    act.wait_ge(S("xt_ps"), k + 1 + r * RUN["xt_ps"])
                    act.activation(xT[p][:, :], banks[p][:, 0:D], ACT.Copy).then_inc(S("xt"), 1)
                    act.wait_ge(S("lo"), k + 1 + r * RUN["lo"])
                    act.wait_ge(S("hi"), k + 1 + r * RUN["hi"])
                    act.sem_inc(S("xh_free"), 1)
                    act.wait_ge(S("dm"), k + 1 + r * RUN["dm"])
                    act.activation(ed[p][:, :], dm[p][:, :], ACT.Exp).then_inc(S("ed"), 1)

        def route_pe(pe, r):
            pe.wait_ge(S("const_in"), 48)
            with pe.Fori(0, NT // 2) as i:
                for p in range(2):
                    k = i * 2 + p
                    pe.wait_ge(S("xh"), k + 1 + r * RUN["xh"])
                    for c in range(KD):
                        m = pe.transpose(banks[p][:, c * P:(c + 1) * P], xh[p][:, c * P:(c + 1) * P], ident)
                    m.then_inc(S("xt_ps"), 1)
                    pe.wait_ge(S("xt"), k + 1 + r * RUN["xt"])
                    for c in range(KD):
                        m = pe.matmul(banks[2 + p][:, 0:E], xT[p][:, c * P:(c + 1) * P], rw[:, c * E:(c + 1) * E],
                                      start=c == 0, stop=c == KD - 1)
                    m.then_inc(S("logit_ps"), 1)
                    pe.wait_ge(S("ohb"), k + 1 + r * RUN["ohb"])
                    pe.wait_ge(S("ohacc"), k + 1 + r * RUN["ohacc"])
                    pe.matmul(banks[4 + p][:, 0:E], before16, ohb[p][:, :], start=True, stop=False)
                    pe.matmul(banks[4 + p][:, 0:E], ones16, ohacc[p][:, :], start=False, stop=True)\
                        .then_inc(S("rank_ps"), 1)
            pe.wait_ge(S("ohacc"), NT + 1 + r * RUN["ohacc"])
            pe.wait_ge(S("slot"), NT + r * RUN["slot"])
            pe.matmul(banks[4][:, 0:E], ones16, ohacc[0][:, :], start=True, stop=True).then_inc(S("count_ps"), 1)

        def route_pool(pool, r):
            if r == 0:
                pool.sem_inc(S("scat_free"), 2)
            with pool.Fori(0, NT // 2) as i:
                for p in range(2):
                    k = i * 2 + p
                    pool.wait_ge(S("slot"), k + 1 + r * RUN["slot"])
                    pool.wait_ge(S("lo"), k + 1 + r * RUN["lo"])
                    hold(pool, "pool")
                    for j in range(2):
                        pool.indirect_dma_start(disp, bass.IndirectOffsetOnAxis(ap=sloti[p][:, j:j + 1], axis=0),
                                                drow[p][:, :], None).then_inc(S(f"scat_{p}"), 16)
                    if p == 1:
                        for q in range(2):
                            pool.wait_ge(S(f"scat_{q}"), i * 32 + 32 + r * RUN["scat"])
                        pool.sem_inc(S("scat_free"), 2)
                        pool.sem_inc(S("drow_free"), 2)
            pool.wait_ge(S("pad"), 1 + r * RUN["pad"])
            pool.wait_ge(S("zrow_set"), 1)
            for e in range(E):
                pool.indirect_dma_start(disp, bass.IndirectOffsetOnAxis(ap=padi[:, e:e + 1], axis=0),
                                        zrow[:, :], None).then_inc(S("padded"), 16)

        def experts_sync(sp, r):
            sp.wait_ge(S("padded"), 16 * E + r * RUN["padded"])
            sp.wait_ge(S("table"), 1 + r * RUN["table"])
            if r == 0:
                sp.sem_inc(S("xin_free"), 2)
            with sp.Fori(0, NS // 2) as i:
                for p in range(2):
                    t = i * 2 + p
                    at = sp.value_load(tabi[0:1, ds(t + NS, 1)], min_val=0, max_val=E * CAP - P)
                    sp.wait_ge(S("xin_free"), t + 1 + r * RUN["xin_free"])
                    sp.dma_start(xin[p][:, :], disp[ds(at, P), :]).then_inc(S(f"xin_{p}"), 16)

        def experts_store(pool, r):
            with pool.Fori(0, NS // 2) as i:
                for p in range(2):
                    t = i * 2 + p
                    pool.wait_ge(S("ysb"), t + 1 + r * RUN["ysb"])
                    pool.dma_start(yrows[ds(t * P, P), :], ysb[p][:, :]).then_inc(S(f"yst_{p}"), 16)

        def experts_pe(pe, r):
            pe.wait_ge(S("table"), 1 + r * RUN["table"])

            def turn(i, p, t):
                pe.wait_ge(S(f"xin_{p}"), i * 16 + 16 + r * RUN["xin"])
                pe.wait_ge(S("xth_free"), t + 1 + r * RUN["xth_free"])
                for c in range(4):
                    m = pe.transpose(banks[p].bitcast(F16)[:, c * P:(c + 1) * P], xin[p][:, c * P:(c + 1) * P], ident16)
                m.then_inc(S("turned"), 1)

            def up(p, t):
                e = pe.value_load(tabi[0:1, ds(t, 1)], min_val=0, max_val=E - 1)
                pe.wait_ge(S("xth"), t + 1 + r * RUN["xth"])
                pe.wait_ge(S("h_free"), t + 1 + r * RUN["h_free"])
                for m in range(KH):
                    o = banks[2 + p][:, m * P:(m + 1) * P]
                    for c in range(KD):
                        hi, lo = xTh[p][:, c * P:(c + 1) * P], xTh[p][:, (KD + c) * P:(KD + c + 1) * P]
                        for n, (w, x) in enumerate((("h", hi), ("h", lo), ("l", hi))):
                            mm = pe.matmul(o, w1[w][:, ds(e * (KD * HID) + (c * HID + m * P), P)], x,
                                           start=c == 0 and n == 0, stop=c == KD - 1 and n == 2)
                mm.then_inc(S("up"), 1)

            def down(p, t):
                e = pe.value_load(tabi[0:1, ds(t, 1)], min_val=0, max_val=E - 1)
                pe.wait_ge(S("hl"), t + 1 + r * RUN["hl"])
                pe.wait_ge(S("y_free"), t + 1 + r * RUN["y_free"])
                o = banks[4 + p][:, 0:D]
                for c in range(KH):
                    hi, lo = hh[p][:, c * P:(c + 1) * P], hl[p][:, c * P:(c + 1) * P]
                    for n, (x, w) in enumerate(((hi, "h"), (hi, "l"), (lo, "h"))):
                        mm = pe.matmul(o, x, w2[w][:, ds(e * (KH * D) + c * D, D)],
                                       start=c == 0 and n == 0, stop=c == KH - 1 and n == 2)
                mm.then_inc(S("down"), 1)

            for q in ("xth_free", "h_free", "y_free") if r == 0 else ():
                pe.sem_inc(S(q), 2)
            turn(0, 0, 0)
            turn(0, 1, 1)
            up(0, 0)
            with pe.Fori(0, NS // 2 - 1) as i:
                turn(i + 1, 0, i * 2 + 2)
                up(1, i * 2 + 1)
                down(0, i * 2)
                turn(i + 1, 1, i * 2 + 3)
                up(0, i * 2 + 2)
                down(1, i * 2 + 1)
            up(1, NS - 1)
            down(0, NS - 2)
            down(1, NS - 1)

        def experts_act(act, r):
            def relu(p, t):
                act.wait_ge(S("up"), t + 1 + r * RUN["up"])
                act.wait_ge(S("hl_free"), t + 1 + r * RUN["hl_free"])
                act.activation(hr[p][:, :], banks[2 + p][:, :], ACT.Relu, scale=1.0 / WSCALE).then_inc(S("hr"), 1)
                act.wait_ge(S("hr"), t + 1 + r * RUN["hr"])
                act.sem_inc(S("h_free"), 1)
                act.wait_ge(S("hh_free"), t + 1 + r * RUN["hh_free"])
                act.activation(hh[p][:, :], hr[p][:, :], ACT.Square).then_inc(S("hh"), 1)

            def yout(p, t, i):
                act.wait_ge(S("down"), t + 1 + r * RUN["down"])
                act.sem_inc(S("hh_free"), 1)
                if not isinstance(i, int) or i:
                    act.wait_ge(S(f"yst_{p}"), i * 16 + r * RUN["yst"])
                act.activation(ysb[p][:, :], banks[4 + p][:, 0:D], ACT.Copy).then_inc(S("ysb"), 1)
                act.wait_ge(S("ysb"), t + 1 + r * RUN["ysb"])
                act.sem_inc(S("y_free"), 1)

            if r == 0:
                act.sem_inc(S("hh_free"), 2)
            if r == 0:
                act.sem_inc(S("hl_free"), 2)
            def pair(i):
                relu(1, i * 2 + 1)
                yout(0, i * 2, i)
                relu(0, i * 2 + 2)
                yout(1, i * 2 + 1, i)

            relu(0, 0)
            pair(0)
            with act.Fori(1, NS // 2 - 1) as i:
                pair(i)
            relu(1, NS - 1)
            yout(0, NS - 2, NS // 2 - 1)
            yout(1, NS - 1, NS // 2 - 1)

        def experts_dve(dve, r):
            def take(p, t):
                dve.wait_ge(S("turned"), t + 1 + r * RUN["turned"])
                dve.sem_inc(S("xin_free"), 1)
                dve.tensor_copy(xTh[p][:, :], banks[p].bitcast(F16)[:, 0:4 * P]).then_inc(S("xth"), 1)

            def low(p, t):
                dve.wait_ge(S("hr"), t + 1 + r * RUN["hr"])
                dve.sem_inc(S("xth_free"), 1)
                dve.tensor_tensor(hq[p][:, :], hr[p][:, :], hr[p][:, :], ALU.mult).then_inc(S("hq"), 1)
                dve.wait_ge(S("hq"), t + 1 + r * RUN["hq"])
                dve.wait_ge(S("hh"), t + 1 + r * RUN["hh"])
                dve.tensor_tensor(hl[p][:, :], hq[p][:, :], hh[p][:, :], ALU.subtract).then_inc(S("hl"), 1)
                dve.wait_ge(S("hl"), t + 1 + r * RUN["hl"])
                dve.sem_inc(S("hl_free"), 1)

            take(0, 0)
            take(1, 1)
            low(0, 0)
            with dve.Fori(0, NS // 2 - 1) as i:
                take(0, i * 2 + 2)
                low(1, i * 2 + 1)
                take(1, i * 2 + 3)
                low(0, i * 2 + 2)
            low(1, NS - 1)

        def combine_pool(pool, r):
            for p in range(2):
                pool.wait_ge(S(f"yst_{p}"), 16 * (NS // 2) + r * RUN["yst"])
            pool.wait_ge(S("slots"), 1 + r * RUN["slots"])
            with pool.Fori(0, NT // 2) as i:
                for p in range(2):
                    k = i * 2 + p
                    pool.wait_ge(S("yg_free"), k + 1 + r * RUN["yg_free"])
                    hold(pool, "pool")
                    pool.tensor_copy(gi[p][:, :], row(slots, k, 2)).then_inc(S("gi"), 1)
                    pool.wait_ge(S("gi"), k + 1 + r * RUN["gi"])
                    hold(pool, "pool")
                    for j in range(2):
                        pool.indirect_dma_start(yg[p][j][:, :], None, yrows,
                                                bass.IndirectOffsetOnAxis(ap=gi[p][:, j:j + 1], axis=0))\
                            .then_inc(S(f"yg_{p}"), 16)

        def combine_dve(dve, r):
            with dve.Fori(0, NT // 2) as i:
                for p in range(2):
                    k = i * 2 + p
                    dve.wait_ge(S(f"yg_{p}"), i * 32 + 32 + r * RUN["yg"])
                    for j in range(2):
                        dve.scalar_tensor_tensor(out=Xk(k), in0=yg[p][j][:, :], scalar=wts[:, ds(k * 2 + j, 1)],
                                                 in1=Xk(k), op0=ALU.mult, op1=ALU.add).then_inc(S("xnew"), 1)
                        dve.wait_ge(S("xnew"), k * 2 + (j + 1) + r * RUN["xnew"])
                    dve.sem_inc(S("yg_free"), 1)

        def vc(i, j=0, n=None):
            return vec[:, V_OFF[i] + j:V_OFF[i] + j + (n or V_W[i])]

        def heads(ap, n):
            return ap.unsqueeze(2).to_broadcast([ap.shape[0], NH, n])

        def by_head(ap):
            return ap.rearrange("p (h e) -> p h e", h=NH)

        def taps(p, lo, n):
            return U[p][:, :].rearrange("p (j b t) -> p j b t", b=B, t=QT + DC - 1)[:, :, :, lo:lo + n]

        def mamba_load(sp):
            for t, name in ((wz, "wz"), (wx, "wx"), (wbc, "wbc"), (wdt, "wdt"), (wo, "wo")):
                sp.dma_start(t[:, :].rearrange("p (c n) -> p c n", n=a[name].shape[1]),
                             a[name].rearrange("(c p) n -> p c n", p=P)).then_inc(S("m_in"), 16)
            sp.dma_start(vec[:, :], a["vectors"]).then_inc(S("m_in"), 16)

        def over_tiles(eng, front, back):
            front(0, 0, 0)
            with eng.Fori(0, NT // 2 - 1) as i:
                for p in range(2):
                    front(i * 2 + (p + 1), 1 - p, i)
                    back(i * 2 + p, p, i)
            front(NT - 1, 1, NT // 2 - 1)
            back(NT - 2, 0, NT // 2 - 1)
            back(NT - 1, 1, NT // 2 - 1)

        def mamba_dve(dve):
            fc = Chain(dve, S("m_front_chain"), 32)
            bc = Chain(dve, S("m_back_chain"), 3)
            dve.wait_ge(S("m_in"), 16 * 6)
            dve.memset(Hs[:, :], 0.0).then_inc(S("m_state"), 1)
            dve.tensor_scalar(negA[:, :], vc(V_AL), A_LOG_MAX, None, ALU.min).then_inc(S("m_alog"), 1)
            dve.wait_ge(S("m_expA"), 1)
            dve.tensor_scalar(negA[:, :], negA[:, :], -1.0, None, ALU.mult).then_inc(S("m_negA"), 1)
            dve.wait_ge(S("m_negA"), 1)

            def front(k, p, i):
                fc.at(k)
                dve.wait_ge(S(f"yg_{p}"), (k - p) * 16 + 32 if isinstance(k, int) else (i if p else i + 1) * 32 + 32)
                for j in range(2):
                    fc.link(dve.scalar_tensor_tensor(out=Xk(k), in0=yg[p][j][:, :], scalar=wts[:, ds(k * 2 + j, 1)],
                                                     in1=Xk(k), op0=ALU.mult, op1=ALU.add))
                dve.sem_inc(S("yg_free"), 1)
                fc.link(dve.bn_stats(ma[:, 0:6], Xk(k)))
                hold(dve, "dve")
                fc.link(dve.bn_aggr(ma[:, 6:8], ma[:, 0:6]))
                dve.tensor_scalar(ma[:, 8:9], ma[:, 7:8], EPS, None, ALU.add).then_inc(S("m_va"), 1)
                dve.wait_ge(S("m_ra"), k + 1)
                fc.link(dve.tensor_scalar(xm[:, :], Xk(k), ma[:, 6:7], ma[:, 9:10], ALU.subtract, ALU.mult))
                fc.link(dve.bn_stats(mb[:, 0:6], xm[:, :]))
                hold(dve, "dve")
                fc.link(dve.bn_aggr(mb[:, 6:8], mb[:, 0:6]))
                dve.tensor_scalar(mb[:, 8:9], mb[:, 7:8], EPS, None, ALU.add).then_inc(S("m_vb"), 1)
                fc.link(dve.tensor_tensor(Xk(k), Xk(k), xm[:, :], ALU.add))
                dve.wait_ge(S("m_rb"), k + 1)
                dve.tensor_scalar(xn[:, :], xm[:, :], mb[:, 6:7], mb[:, 9:10], ALU.subtract, ALU.mult)\
                    .then_inc(S("m_xn"), 1)
                dve.wait_ge(S("m_U"), k + 1)
                dve.wait_ge(S("m_hist"), k + 1)
                for c in range(DC):
                    for j in range(NB + 1):
                        o = cv[:, j * P:(j + 1) * P].rearrange("p (b t) -> p b t", t=QT)
                        u = taps(p, c, QT)[:, j]
                        if c == 0:
                            m = dve.tensor_scalar(o, u, vc(V_CW, j * DC, 1), vc(V_CB, j, 1), ALU.mult, ALU.add)
                        else:
                            dve.wait_ge(S("m_tap"), (k * (DC * (NB + 1))) + ((c - 1) * (NB + 1) + j + 1))
                            m = dve.scalar_tensor_tensor(out=o, in0=u, scalar=vc(V_CW, j * DC + c, 1), in1=o,
                                                         op0=ALU.mult, op1=ALU.add)
                        m.then_inc(S("m_tap"), 1)
                v, nab, e_, den_, s_, s2, q, l = (dv[:, n * NH:(n + 1) * NH] for n in range(8))
                dve.wait_ge(S("m_dtp"), k + 1)
                fc.link(dve.tensor_tensor(v, banks[0][:, 2 * P:2 * P + NH], vc(V_DTB), ALU.add))
                dve.scalar_tensor_tensor(out=nab, in0=v, scalar=-1.0, in1=v, op0=ALU.mult, op1=ALU.min)\
                    .then_inc(S("m_nab"), 1)
                dve.wait_ge(S("m_th"), k + 1)
                fc.link(dve.scalar_tensor_tensor(out=th[:, :], in0=th[:, :], scalar=1.0, in1=cv[:, :],
                                                 op0=ALU.add, op1=ALU.mult))
                n = B * DS_
                dve.tensor_tensor(bm[:, :], th[0:n, NB * P:], const(C_HALF)[0:n, :], ALU.mult).then_inc(S("m_g"), 1)
                dve.tensor_tensor(cm[p][:, :], th[n:2 * n, NB * P:], const(C_HALF)[n:2 * n, :], ALU.mult)\
                    .then_inc(S("m_g"), 1)
                dve.wait_ge(S("m_e"), k + 1)
                fc.link(dve.tensor_scalar(den_, e_, 2.0, None, ALU.add))
                fc.link(dve.reciprocal(den_, den_))
                fc.link(dve.tensor_tensor(s_, e_, den_, ALU.mult))
                fc.link(dve.tensor_tensor(s2, s_, s_, ALU.mult))
                fc.link(dve.tensor_scalar(q, s2, 1.0 / 15, None, ALU.mult))
                for c in (13, 11, 9, 7, 5, 3):
                    fc.link(dve.scalar_tensor_tensor(out=q, in0=q, scalar=1.0 / c, in1=s2, op0=ALU.add, op1=ALU.mult))
                fc.link(dve.scalar_tensor_tensor(out=l, in0=q, scalar=1.0, in1=s_, op0=ALU.add, op1=ALU.mult))
                fc.link(dve.tensor_scalar(v, v, 0.0, None, ALU.max))
                fc.link(dve.scalar_tensor_tensor(out=dt_[p][:, :], in0=l, scalar=2.0, in1=v, op0=ALU.mult, op1=ALU.add))
                dve.wait_ge(S("m_a_free"), k + 1)
                fc.link(dve.scalar_tensor_tensor(out=a_[p][:, :], in0=dt_[p][:, :], scalar=DOWN, in1=negA[:, :],
                                                 op0=ALU.mult, op1=ALU.mult))
                dve.tensor_scalar(a_[p][:, :], a_[p][:, :], CLAMP * DOWN, 1.0 / DOWN, ALU.max, ALU.mult)\
                    .then_inc(S("m_a"), 1)
                dve.wait_ge(S("m_cbp"), k + 1)
                fc.link(dve.tensor_copy(bt[p][:, :], banks[2][:, 0:B * DS_]))
                fc.link(dve.tensor_reduce(cbr[:, :], banks[2][:, P:2 * P].rearrange("p (b t) -> p t b", b=B), AX.X, ALU.add))
                dve.tensor_tensor(cb[p][:, :], cbr[:, :], const(C_QM), ALU.mult).then_inc(S("m_cb"), 1)
                dve.wait_ge(S("m_xs"), k + 1)
                fc.link(dve.tensor_tensor(by_head(dtx[p][:, :]), by_head(xs[p][:, :]), heads(dt_[p][:, :], HP), ALU.mult))
                for b in range(B):
                    m = dve.tensor_scalar(bd[p].rearrange("p (h b e) -> p h b e", b=B, e=HP)[:, :, b, :],
                                          by_head(dtx[p][:, :]), const(C_BM)[:, b:b + 1], None, ALU.mult)
                    fc.link(m)
                dve.sem_inc(S("m_bd"), 1)
                fc.done()

            def back(k, p, i):
                bc.at(k)
                dve.wait_ge(S("m_tz"), k + 1)
                dve.scalar_tensor_tensor(out=gz[:, :], in0=tz[:, :], scalar=1.0, in1=banks[3][:, :],
                                         op0=ALU.add, op1=ALU.mult).then_inc(S("m_gz"), 1)
                dve.wait_ge(S("m_ee"), k + 1)
                dve.tensor_tensor(by_head(dtxw[:, :]), by_head(dtx[p][:, :]), heads(ee[:, NH:2 * NH], HP), ALU.mult)\
                    .then_inc(S("m_dtxw"), 1)
                dve.wait_ge(S("m_inter"), k + 1)
                dve.tensor_tensor(by_head(yi[:, :]), by_head(banks[7][:, :]), heads(ee[:, 0:NH], HP), ALU.mult)\
                    .then_inc(S("m_yi"), 1)
                bc.link(dve.tensor_tensor(by_head(Hs[:, :]), by_head(Hs[:, :]), heads(dd[:, :], HP), ALU.mult))
                dve.wait_ge(S("m_sp"), k + 1)
                dve.tensor_tensor(Hs[:, :], Hs[:, :], banks[7][0:B * DS_, :], ALU.add).then_inc(S("m_state"), 1)
                for g in range(4):
                    c = slice(g * 16 * QT, (g + 1) * 16 * QT)
                    dve.wait_ge(S("m_L"), k * 4 + (g + 1))
                    v = R[p][:, c].rearrange("p (h t) -> p h t", t=QT)
                    dve.tensor_tensor(v, v, cb[p][:, :].unsqueeze(1).to_broadcast([P, 16, QT]), ALU.mult)\
                        .then_inc(S("m_M"), 1)
                dve.wait_ge(S("m_t1"), k + 1)
                bc.link(dve.tensor_tensor(yi[:, :], yi[:, :], xd[:, :], ALU.add))
                dve.wait_ge(S("m_gz"), k + 1)
                dve.tensor_tensor(G[:, :], yi[:, :], gz[:, :], ALU.mult).then_inc(S("m_G"), 1)
                dve.wait_ge(S("m_o"), k + 1)
                dve.wait_ge(S("m_rr"), k + 1)
                bc.link(dve.scalar_tensor_tensor(out=Xk(k), in0=banks[3][:, 0:D], scalar=mss[:, 2:3], in1=Xk(k),
                                                 op0=ALU.mult, op1=ALU.add))
                dve.sem_inc(S("m_x"), 1)
                dve.sem_inc(S("m_bank3_free"), 1)
                bc.done()

            over_tiles(dve, front, back)

        def mamba_pool(pool):
            pool.wait_ge(S("m_in"), 16 * 6)
            pool.wait_ge(S("slots"), 1)
            for p in range(2):
                pool.wait_ge(S(f"yst_{p}"), 16 * (NS // 2))
            pool.memset(taps(1, QT, DC - 1), 0.0).then_inc(S("m_hist_set"), 1)
            pool.sem_inc(S("yg_free"), 2)

            def gather(k, p):
                pool.wait_ge(S("yg_free"), k + 1)
                hold(pool, "pool")
                pool.tensor_copy(gi[p][:, :], row(slots, k, 2)).then_inc(S("gi"), 1)
                pool.wait_ge(S("gi"), k + 1)
                hold(pool, "pool")
                for j in range(2):
                    pool.indirect_dma_start(yg[p][j][:, :], None, yrows,
                                            bass.IndirectOffsetOnAxis(ap=gi[p][:, j:j + 1], axis=0))\
                        .then_inc(S(f"yg_{p}"), 16)

            def power(sem_in, sem_out, ap_in, ap_out, k):
                pool.wait_ge(S(sem_in), k + 1)
                hold(pool, "pool")
                pool.tensor_tensor(ap_out, ap_in, mhalf[:, 0:1], ALU.pow).then_inc(S(sem_out), 1)

            def front(k, p, i):
                if isinstance(k, int) and k == 0:
                    gather(0, 0)
                if not isinstance(k, int) or k < NT - 1:
                    gather(k + 1, 1 - p)
                power("m_va", "m_ra", ma[:, 8:9], ma[:, 9:10], k)
                power("m_vb", "m_rb", mb[:, 8:9], mb[:, 9:10], k)
                pool.wait_ge(S("m_U"), k)if not isinstance(k, int) or k else pool.wait_ge(S("m_hist_set"), 1)
                pool.wait_ge(S("m_th"), k) if not isinstance(k, int) or k else None
                hold(pool, "pool")
                for j in range(NB + 1):
                    m = pool.tensor_copy(taps(p, 0, DC - 1)[:, j], taps(1 - p, QT, DC - 1)[:, j])
                m.then_inc(S("m_hist"), 1)
                pool.wait_ge(S("m_a"), k + 1)
                pool.wait_ge(S("m_R_free"), k + 1)
                m = pool.tensor_tensor(R[p].rearrange("p (h t) -> p h t", t=QT), heads(a_[p][:, :], QT),
                                       const(C_QM).unsqueeze(1).to_broadcast([P, NH, QT]), ALU.mult)
                m.then_inc(S("m_R"), 1)

            def back(k, p, i):
                pool.wait_ge(S("m_xd_free"), k + 1)
                pool.tensor_tensor(by_head(xd[:, :]), by_head(xs[p][:, :]), heads(vc(V_DP), HP), ALU.mult)\
                    .then_inc(S("m_xd"), 1)
                pool.wait_ge(S("m_xd"), k + 1)
                pool.wait_ge(S("m_y2"), k * (16 * NMOVE) + 16 * NMOVE)
                hold(pool, "pool")
                pool.tensor_tensor(xd[:, :], xd[:, :], y2[:, :], ALU.add).then_inc(S("m_t1"), 1)
                pool.wait_ge(S("m_ss"), k + 1)
                hold(pool, "pool")
                pool.tensor_scalar(mss[:, 1:2], mss[:, 0:1], 1.0 / DI, 4.0 * EPS, ALU.mult, ALU.add)\
                    .then_inc(S("m_ms"), 1)
                pool.wait_ge(S("m_rr_free"), k + 1)
                power("m_ms", "m_rr", mss[:, 1:2], mss[:, 2:3], k)

            pool.sem_inc(S("m_R_free"), 2)
            pool.sem_inc(S("m_xd_free"), 1)
            pool.sem_inc(S("m_rr_free"), 1)
            over_tiles(pool, front, back)

        NMOVE = B * 4

        def mamba_sync(sp):
            with sp.Fori(0, NT) as k:
                sp.wait_ge(S("m_y1"), k + 1)
                for j in range(4):
                    for b in range(B):
                        sp.dma_start(y2[b * QT:(b + 1) * QT, j * P:(j + 1) * P], y1[j * QT:(j + 1) * QT, b * P:(b + 1) * P])\
                            .then_inc(S("m_y2"), 16)

        def mamba_act(act):
            act.wait_ge(S("m_in"), 16 * 6)
            act.wait_ge(S("m_alog"), 1)
            act.activation(negA[:, :], negA[:, :], ACT.Exp).then_inc(S("m_expA"), 1)
            act.sem_inc(S("m_xs_free"), 2)
            act.sem_inc(S("m_U_free"), 2)

            def front(k, p, i):
                act.wait_ge(S("m_xT"), k + 1)
                for c in range(KD):
                    m = act.activation(xnT[p][:, c * P:(c + 1) * P], banks[0][:, c * P:(c + 1) * P], ACT.Identity,
                                       scale=vc(V_LNW, c, 1), bias=vc(V_LNB, c, 1))
                m.then_inc(S("m_xnT"), 1)
                act.wait_ge(S("m_up"), k + 1)
                act.wait_ge(S("m_U_free"), k + 1)
                act.activation(taps(p, DC - 1, QT)[:, 0:NB], banks[1][:, :].rearrange("p (j b t) -> p j b t", b=B, t=QT),
                               ACT.Copy).then_inc(S("m_U1"), 1)
                act.activation(taps(p, DC - 1, QT)[:, NB], banks[2][:, 0:P].rearrange("p (b t) -> p b t", t=QT),
                               ACT.Copy).then_inc(S("m_U"), 1)
                act.wait_ge(S("m_nab"), k + 1)
                act.activation(dv[:, 2 * NH:3 * NH], dv[:, NH:2 * NH], ACT.Exp).then_inc(S("m_e"), 1)
                act.wait_ge(S("m_tap"), k * (DC * (NB + 1)) + DC * (NB + 1))
                act.sem_inc(S("m_U_free"), 1)
                act.activation(th[:, :], cv[:, :], ACT.Tanh, scale=0.5).then_inc(S("m_th"), 1)
                act.wait_ge(S("m_xsp"), k + 1)
                act.wait_ge(S("m_xs_free"), k + 1)
                act.activation(xs[p][:, :], banks[6][:, :], ACT.Copy, scale=0.5).then_inc(S("m_xs"), 1)

            def back(k, p, i):
                act.wait_ge(S("m_z"), k + 1)
                act.activation(tz[:, :], banks[3][:, :], ACT.Tanh, scale=0.5).then_inc(S("m_tz"), 1)
                act.wait_ge(S("m_ep"), k + 1)
                act.activation(ee[:, :], banks[0][:, 0:2 * NH], ACT.Exp)
                act.activation(dd[:, :], banks[0][0:B * DS_, 2 * NH:3 * NH], ACT.Exp).then_inc(S("m_ee"), 1)
                for g in range(4):
                    act.wait_ge(S("m_Lp"), k * 4 + (g + 1))
                    act.activation(R[p][:, g * 512:(g + 1) * 512], banks[4 + g % 2][:, :], ACT.Exp).then_inc(S("m_L"), 1)
                act.wait_ge(S("m_intra"), k + 1)
                act.sem_inc(S("m_R_free"), 1)
                act.activation(y1[:, :].rearrange("p (b h e) -> p h b e", b=B, e=HP),
                               banks[6][:, :].rearrange("p (h b e) -> p h b e", b=B, e=HP), ACT.Copy).then_inc(S("m_y1"), 1)
                act.wait_ge(S("m_G"), k + 1)
                act.sem_inc(S("m_xs_free"), 1)
                act.sem_inc(S("m_xd_free"), 1)
                act.activation(tz[:, :], G[:, :], ACT.Square, accum_out=mss[:, 0:1]).then_inc(S("m_ss"), 1)
                act.wait_ge(S("m_GTp"), k + 1)
                for j in range(NB):
                    m = act.activation(GT[:, j * P:(j + 1) * P], banks[1][:, j * P:(j + 1) * P], ACT.Copy,
                                       scale=vc(V_RMS, j, 1))
                m.then_inc(S("m_GT"), 1)
                act.wait_ge(S("m_x"), k + 1)
                act.sem_inc(S("m_rr_free"), 1)

            over_tiles(act, front, back)

        def mamba_pe(pe):
            pe.wait_ge(S("m_in"), 16 * 6)
            pe.sem_inc(S("m_a_free"), 2)
            pe.sem_inc(S("m_bank3_free"), 1)

            def proj(o, w, n, lo, k, xp, tokens_first):
                for c in range(KD):
                    x = xnT[xp][:, c * P:(c + 1) * P]
                    ww = w[:, c * n + lo:c * n + lo + (n if tokens_first else P)]
                    m = pe.matmul(o, x if tokens_first else ww, ww if tokens_first else x, start=c == 0, stop=c == KD - 1)
                return m

            def front(k, p, i):
                first = isinstance(k, int) and k == 0
                pe.wait_ge(S("m_xn"), k + 1)
                if not first:
                    pe.wait_ge(S("m_nab"), k)
                for c in range(KD):
                    m = pe.transpose(banks[0][:, c * P:(c + 1) * P], xn[:, c * P:(c + 1) * P], ident)
                m.then_inc(S("m_xT"), 1)
                pe.wait_ge(S("m_xnT"), k + 1)
                proj(banks[0][:, 2 * P:2 * P + NH], wdt, NH, 0, k, p, True).then_inc(S("m_dtp"), 1)
                if not first:
                    pe.wait_ge(S("m_cb"), k)
                proj(banks[2][:, 0:P], wbc, P, 0, k, p, False)
                for j in range(NB):
                    m = proj(banks[1][:, j * P:(j + 1) * P], wx, DI, j * P, k, p, False)
                m.then_inc(S("m_up"), 1)
                pe.wait_ge(S("m_g"), k * 2 + 2)
                for j in range(NB):
                    m = pe.transpose(banks[6][:, j * P:(j + 1) * P], th[:, j * P:(j + 1) * P], ident)
                m.then_inc(S("m_xsp"), 1)
                n = B * DS_
                pe.wait_ge(S("m_U"), k + 1)
                pe.matmul(banks[2][:, P:2 * P], bm[:, :], cm[p][:, :], start=True, stop=True)
                pe.transpose(banks[2][:, 0:n], bm[:, :], ident[0:n, 0:n]).then_inc(S("m_cbp"), 1)

            def back(k, p, i):
                pe.wait_ge(S("m_bank3_free"), k + 1)
                proj(banks[3][:, :], wz, DI, 0, k, p, True).then_inc(S("m_z"), 1)
                pe.wait_ge(S("m_a"), k + 1)
                if not (isinstance(k, int) and k == NT - 1):
                    pe.wait_ge(S("m_nab"), k + 2)
                pe.matmul(banks[0][:, 0:NH], const(C_INC), a_[p][:, :], start=True, stop=True)
                pe.matmul(banks[0][:, NH:2 * NH], const(C_GT), a_[p][:, :], start=True, stop=True)
                pe.matmul(banks[0][0:B * DS_, 2 * NH:3 * NH], const(C_BLK), a_[p][:, :], start=True, stop=True)\
                    .then_inc(S("m_ep"), 1)
                pe.wait_ge(S("m_state"), k + 1)
                pe.matmul(banks[7][:, :], cm[p][:, :], Hs[:, :], start=True, stop=True).then_inc(S("m_inter"), 1)
                pe.wait_ge(S("m_R"), k + 1)
                for g in range(4):
                    if g >= 2:
                        pe.wait_ge(S("m_L"), k * 4 + (g - 1))
                    pe.matmul(banks[4 + g % 2][:, :], const(C_GT), R[p][:, g * 512:(g + 1) * 512], start=True, stop=True)\
                        .then_inc(S("m_Lp"), 1)
                pe.wait_ge(S("m_L"), k * 4 + 4)
                pe.sem_inc(S("m_a_free"), 1)
                pe.wait_ge(S("m_yi"), k + 1)
                pe.wait_ge(S("m_dtxw"), k + 1)
                pe.matmul(banks[7][0:B * DS_, :], bt[p][:, :], dtxw[:, :], start=True, stop=True).then_inc(S("m_sp"), 1)
                pe.wait_ge(S("m_bd"), k + 1)
                if not (isinstance(k, int) and k == NT - 1):
                    pe.wait_ge(S("m_xs"), k + 2)
                for h in range(NH):
                    j, hh_ = h // 16, h % 16
                    if hh_ == 0:
                        pe.wait_ge(S("m_M"), k * 4 + (j + 1))
                    m = pe.matmul(banks[6][j * QT:(j + 1) * QT, hh_ * B * HP:(hh_ + 1) * B * HP],
                                  R[p][:, h * QT:(h + 1) * QT], bd[p][:, h * B * HP:(h + 1) * B * HP], start=True, stop=True)
                m.then_inc(S("m_intra"), 1)
                pe.wait_ge(S("m_G"), k + 1)
                if not (isinstance(k, int) and k == NT - 1):
                    pe.wait_ge(S("m_U1"), k + 2)
                for j in range(NB):
                    m = pe.transpose(banks[1][:, j * P:(j + 1) * P], G[:, j * P:(j + 1) * P], ident)
                m.then_inc(S("m_GTp"), 1)
                pe.wait_ge(S("m_GT"), k + 1)
                for j in range(NB):
                    m = pe.matmul(banks[3][:, 0:D], GT[:, j * P:(j + 1) * P], wo[:, j * D:(j + 1) * D],
                                  start=j == 0, stop=j == NB - 1)
                m.then_inc(S("m_o"), 1)

            over_tiles(pe, front, back)

        def store_out(sp, r):
            for g in range(4):
                n = NT // 4
                sp.wait_ge(S("xnew"), 2 * n * (g + 1)) if STAGE > 1 else sp.wait_ge(S("m_x"), n * (g + 1))
                for b in range(B):
                    sp.dma_start(out[b].rearrange("(k t) d -> t k d", t=QT)[:, g * n:(g + 1) * n, :],
                                 X[b * QT:(b + 1) * QT, g * n * D:(g + 1) * n * D].rearrange("t (k d) -> t k d", d=D))\
                        .then_inc(S("stored"), 16)
            sp.wait_ge(S("stored"), 16 * B * 4)

        block = ctx.enter_context(nc.Block())

        @block.sync
        def _(sp):
            sync_load(sp)
            mamba_load(sp)
            experts_sync(sp, 0)
            mamba_sync(sp)
            if STAGE > 1:
                experts_sync(sp, 1)
            store_out(sp, 1)

        @block.scalar
        def _(act):
            split_weights(None, act)
            route_act(act, 0)
            experts_act(act, 0)
            mamba_act(act)
            if STAGE > 1:
                route_act(act, 1)
                experts_act(act, 1)

        @block.gpsimd
        def _(pool):
            pool_rstd(pool, 0)
            route_pool(pool, 0)
            experts_store(pool, 0)
            mamba_pool(pool)
            if STAGE > 1:
                pool_rstd(pool, 1)
                route_pool(pool, 1)
                experts_store(pool, 1)
                combine_pool(pool, 1)

        @block.vector
        def _(dve):
            dve.wait_ge(S("x_in"), 16 * B)
            stats(dve, 0)
            split_weights(dve, None)
            route_dve(dve, 0)
            experts_dve(dve, 0)
            mamba_dve(dve)
            if STAGE > 1:
                stats(dve, 1)
                route_dve(dve, 1)
                experts_dve(dve, 1)
                combine_dve(dve, 1)

        @block.tensor
        def _(pe):
            route_pe(pe, 0)
            experts_pe(pe, 0)
            mamba_pe(pe)
            if STAGE > 1:
                route_pe(pe, 1)
                experts_pe(pe, 1)


def constants():
    import numpy as np
    p = np.arange(P)[:, None]
    q = np.arange(P)[None, :]
    same = p // QT == q // QT
    parts = {
        C_ID: p == q,
        C_INC: same & (p <= q),
        C_GT: same & (p > q),
        C_BLK: p // QT == (np.arange(B * DS_)[None, :] // DS_),
        C_HALF: 0.5 * (p % (B * DS_) // DS_ == q // QT),
        C_QM: p % QT <= np.arange(QT)[None, :],
        C_BM: p // QT == np.arange(B)[None, :],
        C_IOTA: np.broadcast_to(np.arange(E)[None, :], (P, E)),
        C_ECAP: np.broadcast_to(CAP * np.arange(E)[None, :], (P, E)),
        C_TRI: p,
        C_TAB: np.broadcast_to(np.arange(NS)[None, :], (P, NS)),
    }
    c32 = np.concatenate([np.asarray(parts[i], np.float32) for i in range(len(C_W))], axis=1)
    c16 = np.concatenate([p == q, p < q, np.ones((P, P), bool)], axis=1).astype(np.float16)
    return np.ascontiguousarray(c32), c16


def kernel(**inputs):
    import numpy as np
    import concourse.bacc as bacc
    from concourse.bass_utils import run_bass_kernel_spmd

    g = {k.replace("L0_", ""): np.asarray(v) for k, v in inputs.items()}
    c32, c16 = constants()
    W = g["attn_W_in"]
    channels = np.concatenate([np.arange(DI), DI + np.arange(2 * DS_).reshape(2, 1, DS_).repeat(B, 1).ravel()])
    cw = g["attn_conv_w"][:, 0, channels].reshape(DC, NB + 1, P).transpose(2, 1, 0).reshape(P, -1)
    cbias = g["attn_conv_b"][channels].reshape(NB + 1, P).T
    rows = [np.broadcast_to(g[n], (P, NH)) for n in ("attn_dt_bias", "attn_Dp", "attn_A_log")]
    vectors = np.concatenate([g["attn_ln_w"].reshape(KD, P).T, g["attn_ln_b"].reshape(KD, P).T, cw, cbias,
                              g["attn_rms_w"].reshape(NB, P).T] + rows, axis=1)
    arrays = {
        "x": g["attn_x"], "router": g["ffn_router_w"].T, "w1": g["ffn_w1"], "w2": g["ffn_w2"],
        "wz": W[:, 0:DI], "wx": W[:, DI:2 * DI],
        "wbc": W[:, 2 * DI:][:, np.arange(2 * DS_).reshape(2, 1, DS_).repeat(B, 1).ravel()],
        "wdt": W[:, -NH:], "wo": g["attn_W_out"], "vectors": vectors,
        "consts": c32, "consts16": c16,
    }
    arrays = {k: np.ascontiguousarray(v) for k, v in arrays.items()}
    nc = bacc.Bacc("TRN2", target_bir_lowering=False, num_devices=1)
    a = {k: nc.dram_tensor(f"in_{k}", v.shape, mybir.dt.from_np(v.dtype), kind="ExternalInput").ap()
         for k, v in arrays.items()}
    out = nc.dram_tensor("out", (B, T, D), F32, kind="ExternalOutput").ap()
    build(nc, a, out)
    r = run_bass_kernel_spmd(nc, [{f"in_{k}": v for k, v in arrays.items()}], core_ids=[0])
    return r.results[0]["out"]
```

```python
import math
from contextlib import ExitStack

import concourse.bass as bass
from concourse import mybir

F32, F16 = mybir.dt.float32, mybir.dt.float16
U32, I32 = mybir.dt.uint32, mybir.dt.int32
ALU = mybir.AluOpType
ACT = mybir.ActivationFunctionType
AX = mybir.AxisListType
ds = bass.ds

P = 128
B, T, D = 4, 1024, 256
E, HID = 8, 512
QT = P // B
NT = B * T // P
KD, KH = D // P, HID // P
CAP = B * T + P
NS = 2 * NT + E
WSCALE = 64.0
EPS = 1e-5
DI, DS_, DC, NH = 512, 16, 4, 64
HP = DI // NH
NB = DI // P

C_ID, C_INC, C_GT, C_BLK, C_HALF, C_QM, C_BM, C_IOTA, C_ECAP, C_TRI, C_TAB = range(11)
NROW = 4
ARENA = 8 * 1024
CLAMP = -110.0
DOWN = 2.0 ** -20
A_LOG_MAX = 88.0
C_W = [P, P, P, B * DS_, P, QT, B, E, E, 1, NS]
C_OFF = [sum(C_W[:i]) for i in range(len(C_W) + 1)]


V_LNW, V_LNB, V_CW, V_CB, V_RMS, V_DTB, V_DP, V_AL = range(8)
V_W = [KD, KD, (NB + 1) * DC, NB + 1, NB, NH, NH, NH]
V_OFF = [sum(V_W[:i]) for i in range(len(V_W) + 1)]


RUN = dict.fromkeys(("var", "rstd", "count_ps", "pad", "table", "slots"), 1)
RUN |= dict.fromkeys(("xh", "xh_free", "hi", "lo", "logit_ps", "dm", "ohb", "rank_ps", "scat_free", "ed", "xt_ps", "xt",
                      "slot", "drow_free", "yg_free", "gi"), NT)
RUN |= dict.fromkeys(("turned", "xin_free", "xth", "xth_free", "up", "h_free", "hr", "hq", "hh", "hh_free", "hl", "hl_free",
                      "down", "y_free", "ysb"), NS)
RUN |= {"ohacc": NT + 1, "padded": 16 * E, "scat": 32 * NT // NROW, "xin": 8 * NS, "yst": 8 * NS, "yg": 16 * NT, "xnew": 0}
TABLE_STEPS = 43


class Chain:

    def __init__(self, eng, sem, per_tile, before=0):
        self.eng, self.sem, self.per, self.before = eng, sem, per_tile, before

    def at(self, tile):
        self.base, self.n = tile * self.per + self.before * self.per, 0

    def link(self, ins):
        self.n += 1
        ins.then_inc(self.sem, 1)
        self.eng.wait_ge(self.sem, self.base + self.n)

    def done(self):
        assert self.n == self.per, (self.n, self.per)


def build(nc, a, out):
    with ExitStack() as ctx:
        def sb(name, shape, dt=F32):
            return ctx.enter_context(nc.sbuf_tensor(name, shape, dt))

        def sem(name):
            return ctx.enter_context(nc.semaphore(name))

        banks = [ctx.enter_context(nc.psum_tensor(f"bank{i}", [P, 512], F32)) for i in range(8)]

        X = sb("X", [P, NT * D])
        w1 = {h: sb(f"w1{h}", [P, E * KD * HID], F16) for h in "hl"}
        w2 = {h: sb(f"w2{h}", [P, E * KH * D], F16) for h in "hl"}
        rw = sb("rw", [P, KD * E])
        cst = sb("cst", [P, C_OFF[-1]])
        cst16 = sb("cst16", [P, 3 * P], F16)

        def const(i, n=None):
            return cst[:, C_OFF[i]:C_OFF[i] + (n or C_W[i])]

        ident = const(C_ID)
        ident16, before16, ones16 = (cst16[:, i * P:(i + 1) * P] for i in range(3))
        mv = sb("mv", [P, 2 * NT])
        var = sb("var", [P, NT])
        rstd = sb("rstd", [P, NT])
        mhalf = sb("mhalf", [P, NT])

        disp = nc.dram_tensor("disp", (E * CAP, 2 * D), F16, kind="Internal").ap()
        yrows = nc.dram_tensor("yrows", (NS * P, D), F32, kind="Internal").ap()

        arena = sb("arena", [P, ARENA])
        used = [0]

        def carve(cols, dt=F32, rows=P):
            n = cols * (1 if dt != F16 else 0) or cols // 2
            at, used[0] = used[0], used[0] + n
            assert used[0] <= ARENA, used[0]
            v = arena[0:rows, at:at + n]
            return v if dt == F32 else v.bitcast(dt)

        xh = [carve(D) for p in range(2)]
        drow = [carve(2 * D, F16) for p in range(NROW)]
        xT = [carve(D) for p in range(2)]
        lg = [sb(f"lg{p}", [P, E]) for p in range(2)]
        mx = [sb(f"mx{p}", [P, E]) for p in range(2)]
        ix = [sb(f"ix{p}", [P, E], U32) for p in range(2)]
        ixf = [sb(f"ixf{p}", [P, 2]) for p in range(2)]
        oh = [sb(f"oh{p}", [P, 2 * E]) for p in range(2)]
        ohb = [sb(f"ohb{p}", [P, E], F16) for p in range(2)]
        ohacc = [sb(f"ohacc{p}", [P, E], F16) for p in range(2)]
        dm = [sb(f"dm{p}", [P, 1]) for p in range(2)]
        ed = [sb(f"ed{p}", [P, 1]) for p in range(2)]
        den = [sb(f"den{p}", [P, 2]) for p in range(2)]
        rk = [sb(f"rk{p}", [P, E]) for p in range(2)]
        junk = sb("junk", [P, 2 * E])
        slotf = [sb(f"slotf{p}", [P, 2]) for p in range(2)]
        sloti = [sb(f"sloti{p}", [P, 2], U32) for p in range(NROW)]
        slots = sb("slots", [P, 2 * NT], U32)
        slotd = sb("slotd", [P, 2 * NT])
        eidx = sb("eidx", [P, 2 * NT])
        eadd = sb("eadd", [P, 2 * NT])
        shift = sb("shift", [P, E])
        wts = sb("wts", [P, 2 * NT])
        zrow = sb("zrow", [P, 2 * D], F16)
        cnt = sb("cnt", [P, E])
        pade = sb("pade", [P, E])
        padi = sb("padi", [P, E], U32)
        nti = sb("nti", [P, E], I32)
        ntf = sb("ntf", [P, 2 * E])
        cum = sb("cum", [P, E])
        skip = sb("skip", [P, E])
        tcl = sb("tcl", [1, NS])
        past = sb("past", [1, NS * E])
        tabf = sb("tabf", [1, 2 * NS])
        tabi = sb("tabi", [1, 2 * NS], I32)
        route_end = used[0]
        xin = [carve(2 * D, F16) for p in range(2)]
        xTh = [carve(4 * P, F16) for p in range(2)]
        hr = [carve(HID) for p in range(2)]
        hq = [carve(HID) for p in range(2)]
        hh = [carve(HID, F16) for p in range(2)]
        hl = [carve(HID, F16) for p in range(2)]
        ysb = [carve(D) for p in range(2)]
        used[0] = route_end
        stage = [carve(2048) for p in range(2)]
        gi = [sb(f"gi{p}", [P, 2], U32) for p in range(2)]
        yg = [[sb(f"yg{p}{j}", [P, D]) for j in range(2)] for p in range(2)]
        mv1 = [sb(f"mv1{p}", [P, 2]) for p in range(2)]
        st = [sb(f"st{p}", [P, 6]) for p in range(2)]

        used[0] = 0
        R = [carve(NH * QT) for p in range(2)]
        bd = carve(NH * B * HP)
        wz = sb("wz", [P, KD * DI])
        wx = sb("wx", [P, KD * DI])
        wbc = sb("wbc", [P, KD * P])
        wdt = sb("wdt", [P, KD * NH])
        wo = sb("wo", [P, NB * D])
        vec = sb("vec", [P, V_OFF[-1]])
        negA = sb("negA", [P, NH])
        xm = sb("xm", [P, D])
        xn = sb("xn", [P, D])
        xnT = [sb(f"xnT{p}", [P, D]) for p in range(2)]
        U = [sb(f"U{p}", [P, (NB + 1) * B * (QT + DC - 1)]) for p in range(2)]
        cv = sb("cv", [P, (NB + 1) * P])
        th = sb("th", [P, (NB + 1) * P])
        bm = sb("bm", [B * DS_, P])
        cm = [sb(f"cm{p}", [B * DS_, P]) for p in range(2)]
        bt = [sb(f"bt{p}", [P, B * DS_]) for p in range(2)]
        cbr = sb("cbr", [P, QT])
        cb = [sb(f"cb{p}", [P, QT]) for p in range(2)]
        xs = [sb(f"xs{p}", [P, DI]) for p in range(2)]
        dtx = [sb(f"dtx{p}", [P, DI]) for p in range(2)]
        dv = sb("dv", [P, 8 * NH])
        dt_ = [sb(f"dt{p}", [P, NH]) for p in range(2)]
        a_ = [sb(f"a{p}", [P, NH]) for p in range(2)]
        ee = sb("ee", [P, 2 * NH])
        dd = sb("dd", [B * DS_, NH])
        Hs = sb("Hs", [B * DS_, DI])
        dtxw = sb("dtxw", [P, DI])
        yi = [sb(f"yi{p}", [P, DI]) for p in range(2)]
        y1 = sb("y1", [P, DI])
        y2 = sb("y2", [P, DI])
        tz = sb("tz", [P, DI])
        gz = [sb(f"gz{p}", [P, DI]) for p in range(2)]
        G = sb("G", [P, DI])
        GT = carve(DI)
        xd = carve(DI)
        ma = sb("ma", [P, 6 + 2 + 2])
        mb = sb("mb", [P, 6 + 2 + 2])
        mss = sb("mss", [P, 3])

        s = {}

        def S(name):
            if name not in s:
                s[name] = sem(name)
            return s[name]

        def hold(eng, name):
            eng.sem_inc(S(f"held_{name}"), 1)

        def Xk(k):
            return X[:, ds(k * D, D)] if not isinstance(k, int) else X[:, k * D:(k + 1) * D]

        def row(t, k, n):
            return t[:, ds(k * n, n)]

        xv = a["x"].rearrange("b (k t) d -> k b t d", t=QT)
        ov = out.rearrange("b (k t) d -> k b t d", t=QT)
        NCHUNK = E * KD * HID // 2048

        def sync_load(sp):
            sp.dma_start(cst[:, :], a["consts"]).then_inc(S("const_in"), 16)
            sp.dma_start(cst16[:, :], a["consts16"]).then_inc(S("const_in"), 16)
            sp.dma_start(rw[:, :], a["router"].rearrange("(c p) e -> p c e", p=P)).then_inc(S("const_in"), 16)
            for b in range(B):
                sp.dma_start(X[b * QT:(b + 1) * QT, :].rearrange("t (k d) -> t k d", d=D),
                             a["x"][b].rearrange("(k t) d -> t k d", t=QT)).then_inc(S("x_in"), 16)
            views = ([a["w1"][e].rearrange("(c p) h -> p c h", p=P) for e in range(E)],
                     [a["w2"][e].rearrange("(c p) d -> p c d", p=P) for e in range(E)])
            n = 0
            for v in views:
                for c in range(NCHUNK):
                    if n >= 2:
                        sp.wait_ge(S("stage_used"), n - 1)
                    for j in range(2):
                        sp.dma_start(stage[n % 2][:, j * 1024:(j + 1) * 1024].rearrange("p (c h) -> p c h", c=v[0].shape[1]),
                                     v[2 * c + j]).then_inc(S(f"stage_in{n % 2}"), 16)
                    n += 1

        def split_weights(dve, act):
            n = 0
            for w in (w1, w2):
                for c in range(NCHUNK):
                    hi, lo = (w[h][:, c * 2048:(c + 1) * 2048] for h in "hl")
                    if act:
                        act.wait_ge(S(f"stage_in{n % 2}"), 32 * (n // 2 + 1))
                        act.activation(hi, stage[n % 2][:, :], ACT.Copy, scale=WSCALE).then_inc(S("high_done"), 1)
                    else:
                        dve.wait_ge(S("high_done"), n + 1)
                        dve.scalar_tensor_tensor(out=lo, in0=stage[n % 2][:, :], scalar=WSCALE, in1=hi,
                                                 op0=ALU.mult, op1=ALU.subtract).then_inc(S("stage_used"), 1)
                    n += 1

        def stats(dve, r):
            ch = Chain(dve, S("stats_chain"), 3, r * NT)
            with dve.Fori(0, NT // 2) as i:
                for p in range(2):
                    k = i * 2 + p
                    ch.at(k)
                    ch.link(dve.bn_stats(st[p][:, :], Xk(k)))
                    hold(dve, "dve")
                    ch.link(dve.bn_aggr(mv1[p][:, :], st[p][:, :]))
                    ch.link(dve.tensor_copy(row(mv, k, 2), mv1[p][:, :]))
                    ch.done()
            v = mv[:, :].rearrange("p (k two) -> p k two", two=2)[:, :, 1]
            dve.tensor_scalar(var[:, :], v, EPS, None, ALU.add).then_inc(S("var"), 1)

        def pool_rstd(pool, r):
            if r == 0:
                pool.memset(mhalf[:, :], -0.5).then_inc(S("mhalf_set"), 1)
                pool.memset(zrow[:, :], 0.0).then_inc(S("zrow_set"), 1)
            pool.wait_ge(S("mhalf_set"), 1)
            pool.wait_ge(S("var"), 1 + r * RUN["var"])
            pool.tensor_tensor(rstd[:, :], var[:, :], mhalf[:, :], ALU.pow).then_inc(S("rstd"), 1)

        def route_dve(dve, r):
            ch = Chain(dve, S("route_chain"), 14, r * NT)
            dve.wait_ge(S("rstd"), 1 + r * RUN["rstd"])
            dve.memset(ohacc[0][:, :], 0.0).then_inc(S("ohacc"), 1)
            dve.wait_ge(S("const_in"), 48)
            if r == 0:
                dve.sem_inc(S("xh_free"), 2)
            def norm(k, p):
                dve.wait_ge(S("xh_free"), k + 1 + r * RUN["xh_free"])
                dve.tensor_scalar(xh[p][:, :], Xk(k), row(mv, k, 2)[:, 0:1], row(rstd, k, 1),
                                  ALU.subtract, ALU.mult).then_inc(S("xh"), 1)

            def low(k, q):
                p = q % 2
                dve.wait_ge(S("hi"), k + 1 + r * RUN["hi"])
                dve.tensor_tensor(drow[q][:, D:2 * D], xh[p][:, :], drow[q][:, 0:D], ALU.subtract)\
                    .then_inc(S("lo"), 1)

            def choose(k, q, more=True):
                p = q % 2
                ch.at(k)
                dve.wait_ge(S("logit_ps"), k + 1 + r * RUN["logit_ps"])
                ch.link(dve.tensor_copy(lg[p][:, :], banks[2 + p][:, 0:E]))
                hold(dve, "dve")
                ch.link(dve.max(out=mx[p][:, :], in_=lg[p][:, :]))
                dve.tensor_tensor(dm[p][:, :], mx[p][:, 1:2], mx[p][:, 0:1], ALU.subtract).then_inc(S("dm"), 1)
                hold(dve, "dve")
                ch.link(dve.max_index(ix[p][:, :], mx[p][:, :], lg[p][:, :]))
                ch.link(dve.tensor_copy(ixf[p][:, :], ix[p][:, 0:2]))
                for j in range(2):
                    ch.link(dve.tensor_scalar(oh[p][:, j * E:(j + 1) * E], const(C_IOTA), ixf[p][:, j:j + 1], None,
                                              ALU.is_equal))
                dve.tensor_tensor(ohb[p][:, :], oh[p][:, 0:E], oh[p][:, E:2 * E], ALU.add).then_inc(S("ohb"), 1)
                if more:
                    low(k + 1, (q + 1) % NROW)
                dve.wait_ge(S("ohb"), k + 1 + r * RUN["ohb"])
                dve.wait_ge(S("ohacc"), k + 1 + r * RUN["ohacc"])
                dve.wait_ge(S("rank_ps"), k + 1 + r * RUN["rank_ps"])
                dve.tensor_tensor(ohacc[1 - p][:, :], ohacc[p][:, :], ohb[p][:, :], ALU.add)\
                    .then_inc(S("ohacc"), 1)
                ch.link(dve.tensor_tensor(rk[p][:, :], banks[4 + p][:, 0:E], const(C_ECAP), ALU.add))
                ch.link(dve.tensor_tensor_reduce(junk[:, 0:E], rk[p][:, :], oh[p][:, 0:E], 1.0, 0.0, ALU.mult,
                                                 ALU.add, slotf[p][:, 0:1]))
                ch.link(dve.tensor_tensor_reduce(junk[:, E:2 * E], rk[p][:, :], oh[p][:, E:2 * E], 1.0, 0.0,
                                                 ALU.mult, ALU.add, slotf[p][:, 1:2]))
                dve.wait_ge(S("scat_free"), k + 1 + r * RUN["scat_free"])
                ch.link(dve.tensor_copy(row(slotd, k, 2), slotf[p][:, :]))
                ch.link(dve.tensor_copy(row(eidx, k, 2), ixf[p][:, :]))
                dve.tensor_copy(sloti[q][:, :], slotf[p][:, :]).then_inc(S("slot"), 1)
                dve.wait_ge(S("ed"), k + 1 + r * RUN["ed"])
                ch.link(dve.tensor_scalar(den[p][:, 0:1], ed[p][:, :], 1.0, 2.0 * WSCALE, ALU.add, ALU.mult))
                ch.link(dve.reciprocal(row(wts, k * 2, 1), den[p][:, 0:1]))
                ch.link(dve.tensor_tensor(wts[:, ds(k * 2 + 1, 1)], row(wts, k * 2, 1), ed[p][:, :], ALU.mult))
                ch.done()
            def step(i, q):
                norm(i * NROW + q + 1, (q + 1) % 2)
                choose(i * NROW + q, q)

            norm(0, 0)
            low(0, 0)
            with dve.Fori(0, NT // NROW - 1) as i:
                for q in range(NROW):
                    step(i, q)
            for q in range(NROW - 1):
                step(NT // NROW - 1, q)
            choose(NT - 1, NROW - 1, False)
            dve.wait_ge(S("count_ps"), 1 + r * RUN["count_ps"])
            c2 = Chain(dve, S("table_chain"), TABLE_STEPS, r)
            c2.at(0)
            c2.link(dve.tensor_copy(cnt[:, :], banks[4][:, 0:E]))
            c2.link(dve.tensor_tensor(pade[:, :], cnt[:, :], const(C_ECAP), ALU.add))
            c2.link(dve.tensor_scalar(pade[:, :], pade[:, :], const(C_TRI), None, ALU.add))
            c2.link(dve.tensor_copy(padi[:, :], pade[:, :]))
            dve.sem_inc(S("pad"), 1)
            c2.link(dve.tensor_scalar(ntf[:, 0:E], cnt[:, :], float(P - 1), None, ALU.add))
            c2.link(dve.tensor_copy(nti[:, :], ntf[:, 0:E]))
            c2.link(dve.tensor_scalar(nti[:, :], nti[:, :], int(math.log2(P)), None, ALU.arith_shift_right))
            c2.link(dve.tensor_copy(ntf[:, 0:E], nti[:, :]))
            c2.link(dve.tensor_copy(cum[:, 0:1], ntf[:, 0:1]))
            for e in range(1, E):
                c2.link(dve.tensor_tensor(cum[:, e:e + 1], cum[:, e - 1:e], ntf[:, e:e + 1], ALU.add))
            c2.link(dve.tensor_scalar(skip[:, :], ntf[:, 0:E], -float(P), float(CAP), ALU.mult, ALU.add))
            c2.link(dve.tensor_scalar(ntf[:, E:E + 1], cum[:, E - 1:E], -1.0, None, ALU.add))
            c2.link(dve.tensor_scalar(tcl[:, :], cst[0:1, C_OFF[C_TAB]:C_OFF[C_TAB] + NS], ntf[0:1, E:E + 1], None, ALU.min))
            pv = past[:, :].rearrange("o (t e) -> o t e", e=E)
            c2.link(dve.tensor_tensor(pv, tcl[:, :].unsqueeze(2).to_broadcast([1, NS, E]),
                                      cum[0:1, :].unsqueeze(1).to_broadcast([1, NS, E]), ALU.is_ge))
            c2.link(dve.tensor_reduce(tabf[:, 0:NS], pv, AX.X, ALU.add))
            c2.link(dve.tensor_tensor(pv, pv, skip[0:1, :].unsqueeze(1).to_broadcast([1, NS, E]), ALU.mult))
            c2.link(dve.tensor_reduce(tabf[:, NS:2 * NS], pv, AX.X, ALU.add))
            c2.link(dve.scalar_tensor_tensor(out=tabf[:, NS:2 * NS], in0=tcl[:, :], scalar=float(P),
                                             in1=tabf[:, NS:2 * NS], op0=ALU.mult, op1=ALU.add))
            c2.link(dve.tensor_copy(tabi[:, :], tabf[:, :]))
            dve.sem_inc(S("table"), 1)
            c2.link(dve.tensor_tensor(shift[:, :], cum[:, :], ntf[:, 0:E], ALU.subtract))
            c2.link(dve.scalar_tensor_tensor(out=shift[:, :], in0=shift[:, :], scalar=float(P), in1=const(C_ECAP),
                                             op0=ALU.mult, op1=ALU.subtract))
            for e in range(E):
                c2.link(dve.tensor_scalar(eadd[:, :], eidx[:, :], float(e), shift[:, e:e + 1], ALU.is_equal, ALU.mult))
                c2.link(dve.tensor_tensor(slotd[:, :], slotd[:, :], eadd[:, :], ALU.add))
            dve.tensor_copy(slots[:, :], slotd[:, :]).then_inc(S("slots"), 1)
            c2.done()

        def route_act(act, r):
            if r == 0:
                act.sem_inc(S("drow_free"), NROW)

            def rows(k, q):
                p = q % 2
                act.wait_ge(S("xh"), k + 1 + r * RUN["xh"])
                act.wait_ge(S("drow_free"), k + 1 + r * RUN["drow_free"])
                act.activation(drow[q][:, 0:D], xh[p][:, :], ACT.Copy).then_inc(S("hi"), 1)
                act.wait_ge(S("xt_ps"), k + 1 + r * RUN["xt_ps"])
                act.activation(xT[p][:, :], banks[p][:, 0:D], ACT.Copy).then_inc(S("xt"), 1)

            def used(k):
                act.wait_ge(S("lo"), k + 1 + r * RUN["lo"])
                act.wait_ge(S("hi"), k + 1 + r * RUN["hi"])
                act.sem_inc(S("xh_free"), 1)

            def ratio(k, q):
                act.wait_ge(S("dm"), k + 1 + r * RUN["dm"])
                act.activation(ed[q % 2][:, :], dm[q % 2][:, :], ACT.Exp).then_inc(S("ed"), 1)

            def step(i, q):
                k = i * NROW + q
                rows(k + 1, (q + 1) % NROW)
                ratio(k, q)
                used(k + 1)

            rows(0, 0)
            used(0)
            with act.Fori(0, NT // NROW - 1) as i:
                for q in range(NROW):
                    step(i, q)
            for q in range(NROW - 1):
                step(NT // NROW - 1, q)
            ratio(NT - 1, NROW - 1)

        def route_pe(pe, r):
            pe.wait_ge(S("const_in"), 48)
            def logits(k, p):
                pe.wait_ge(S("xh"), k + 1 + r * RUN["xh"])
                for c in range(KD):
                    m = pe.transpose(banks[p][:, c * P:(c + 1) * P], xh[p][:, c * P:(c + 1) * P], ident)
                m.then_inc(S("xt_ps"), 1)
                pe.wait_ge(S("xt"), k + 1 + r * RUN["xt"])
                for c in range(KD):
                    m = pe.matmul(banks[2 + p][:, 0:E], xT[p][:, c * P:(c + 1) * P], rw[:, c * E:(c + 1) * E],
                                  start=c == 0, stop=c == KD - 1)
                m.then_inc(S("logit_ps"), 1)

            def ranks(k, p):
                pe.wait_ge(S("ohb"), k + 1 + r * RUN["ohb"])
                pe.wait_ge(S("ohacc"), k + 1 + r * RUN["ohacc"])
                pe.matmul(banks[4 + p][:, 0:E], before16, ohb[p][:, :], start=True, stop=False)
                pe.matmul(banks[4 + p][:, 0:E], ones16, ohacc[p][:, :], start=False, stop=True)\
                    .then_inc(S("rank_ps"), 1)

            logits(0, 0)
            with pe.Fori(0, NT // 2 - 1) as i:
                for p in range(2):
                    logits(i * 2 + p + 1, 1 - p)
                    ranks(i * 2 + p, p)
            logits(NT - 1, 1)
            ranks(NT - 2, 0)
            ranks(NT - 1, 1)
            pe.wait_ge(S("ohacc"), NT + 1 + r * RUN["ohacc"])
            pe.wait_ge(S("slot"), NT + r * RUN["slot"])
            pe.matmul(banks[4][:, 0:E], ones16, ohacc[0][:, :], start=True, stop=True).then_inc(S("count_ps"), 1)

        def route_pool(pool, r):
            if r == 0:
                pool.sem_inc(S("scat_free"), NROW)

            def sent(i, q):
                pool.wait_ge(S(f"scat_{q}"), i * 32 + 32 + r * RUN["scat"])
                pool.sem_inc(S("scat_free"), 1)
                pool.sem_inc(S("drow_free"), 1)

            def send(i, q):
                k = i * NROW + q
                pool.wait_ge(S("slot"), k + 1 + r * RUN["slot"])
                pool.wait_ge(S("lo"), k + 1 + r * RUN["lo"])
                hold(pool, "pool")
                for j in range(2):
                    pool.indirect_dma_start(disp, bass.IndirectOffsetOnAxis(ap=sloti[q][:, j:j + 1], axis=0),
                                            drow[q][:, :], None).then_inc(S(f"scat_{q}"), 16)
                if q >= 2:
                    sent(i, q - 2)
                elif not isinstance(i, int):
                    sent(i - 1, q + 2)

            for q in range(NROW):
                send(0, q)
            with pool.Fori(1, NT // NROW) as i:
                for q in range(NROW):
                    send(i, q)
            for q in (NROW - 2, NROW - 1):
                sent(NT // NROW - 1, q)
            pool.wait_ge(S("pad"), 1 + r * RUN["pad"])
            pool.wait_ge(S("zrow_set"), 1)
            for e in range(E):
                pool.indirect_dma_start(disp, bass.IndirectOffsetOnAxis(ap=padi[:, e:e + 1], axis=0),
                                        zrow[:, :], None).then_inc(S("padded"), 16)

        def experts_sync(sp, r):
            sp.wait_ge(S("padded"), 16 * E + r * RUN["padded"])
            sp.wait_ge(S("table"), 1 + r * RUN["table"])
            if r == 0:
                sp.sem_inc(S("xin_free"), 2)
            with sp.Fori(0, NS // 2) as i:
                for p in range(2):
                    t = i * 2 + p
                    at = sp.value_load(tabi[0:1, ds(t + NS, 1)], min_val=0, max_val=E * CAP - P)
                    sp.wait_ge(S("xin_free"), t + 1 + r * RUN["xin_free"])
                    sp.dma_start(xin[p][:, :], disp[ds(at, P), :]).then_inc(S(f"xin_{p}"), 16)

        def experts_store(pool, r):
            with pool.Fori(0, NS // 2) as i:
                for p in range(2):
                    t = i * 2 + p
                    pool.wait_ge(S("ysb"), t + 1 + r * RUN["ysb"])
                    pool.dma_start(yrows[ds(t * P, P), :], ysb[p][:, :]).then_inc(S(f"yst_{p}"), 16)

        def experts_pe(pe, r):
            pe.wait_ge(S("table"), 1 + r * RUN["table"])

            def turn(i, p, t):
                pe.wait_ge(S(f"xin_{p}"), i * 16 + 16 + r * RUN["xin"])
                pe.wait_ge(S("xth_free"), t + 1 + r * RUN["xth_free"])
                for c in range(4):
                    m = pe.transpose(banks[p].bitcast(F16)[:, c * P:(c + 1) * P], xin[p][:, c * P:(c + 1) * P], ident16)
                m.then_inc(S("turned"), 1)

            def expert(t):
                return pe.value_load(tabi[0:1, ds(t, 1)], min_val=0, max_val=E - 1)

            def up(p, t, e):
                pe.wait_ge(S("xth"), t + 1 + r * RUN["xth"])
                pe.wait_ge(S("h_free"), t + 1 + r * RUN["h_free"])
                for m in range(KH):
                    o = banks[2 + p][:, m * P:(m + 1) * P]
                    for c in range(KD):
                        hi, lo = xTh[p][:, c * P:(c + 1) * P], xTh[p][:, (KD + c) * P:(KD + c + 1) * P]
                        for n, (w, x) in enumerate((("h", hi), ("h", lo), ("l", hi))):
                            mm = pe.matmul(o, w1[w][:, ds(e * (KD * HID) + (c * HID + m * P), P)], x,
                                           start=c == 0 and n == 0, stop=c == KD - 1 and n == 2)
                mm.then_inc(S("up"), 1)

            def down(p, t, e):
                pe.wait_ge(S("hl"), t + 1 + r * RUN["hl"])
                pe.wait_ge(S("y_free"), t + 1 + r * RUN["y_free"])
                o = banks[4 + p][:, 0:D]
                for c in range(KH):
                    hi, lo = hh[p][:, c * P:(c + 1) * P], hl[p][:, c * P:(c + 1) * P]
                    for n, (x, w) in enumerate(((hi, "h"), (hi, "l"), (lo, "h"))):
                        mm = pe.matmul(o, x, w2[w][:, ds(e * (KH * D) + c * D, D)],
                                       start=c == 0 and n == 0, stop=c == KH - 1 and n == 2)
                mm.then_inc(S("down"), 1)

            for q in ("xth_free", "h_free", "y_free") if r == 0 else ():
                pe.sem_inc(S(q), 2)
            turn(0, 0, 0)
            turn(0, 1, 1)
            up(0, 0, expert(0))
            with pe.Fori(0, NS // 2 - 1) as i:
                e0, e1, e2 = (expert(i * 2 + n) for n in range(3))
                turn(i + 1, 0, i * 2 + 2)
                up(1, i * 2 + 1, e1)
                down(0, i * 2, e0)
                turn(i + 1, 1, i * 2 + 3)
                up(0, i * 2 + 2, e2)
                down(1, i * 2 + 1, e1)
            e0, e1 = expert(NS - 2), expert(NS - 1)
            up(1, NS - 1, e1)
            down(0, NS - 2, e0)
            down(1, NS - 1, e1)

        def experts_act(act, r):
            def relu(p, t):
                act.wait_ge(S("up"), t + 1 + r * RUN["up"])
                act.wait_ge(S("hl_free"), t + 1 + r * RUN["hl_free"])
                act.activation(hr[p][:, :], banks[2 + p][:, :], ACT.Relu, scale=1.0 / WSCALE).then_inc(S("hr"), 1)
                act.wait_ge(S("hr"), t + 1 + r * RUN["hr"])
                act.sem_inc(S("h_free"), 1)
                act.wait_ge(S("hh_free"), t + 1 + r * RUN["hh_free"])
                act.activation(hh[p][:, :], hr[p][:, :], ACT.Square).then_inc(S("hh"), 1)

            def yout(p, t, i):
                act.wait_ge(S("down"), t + 1 + r * RUN["down"])
                act.sem_inc(S("hh_free"), 1)
                if not isinstance(i, int) or i:
                    act.wait_ge(S(f"yst_{p}"), i * 16 + r * RUN["yst"])
                act.activation(ysb[p][:, :], banks[4 + p][:, 0:D], ACT.Copy).then_inc(S("ysb"), 1)
                act.wait_ge(S("ysb"), t + 1 + r * RUN["ysb"])
                act.sem_inc(S("y_free"), 1)

            if r == 0:
                act.sem_inc(S("hh_free"), 2)
            if r == 0:
                act.sem_inc(S("hl_free"), 2)
            def pair(i):
                relu(1, i * 2 + 1)
                yout(0, i * 2, i)
                relu(0, i * 2 + 2)
                yout(1, i * 2 + 1, i)

            relu(0, 0)
            pair(0)
            with act.Fori(1, NS // 2 - 1) as i:
                pair(i)
            relu(1, NS - 1)
            yout(0, NS - 2, NS // 2 - 1)
            yout(1, NS - 1, NS // 2 - 1)

        def experts_dve(dve, r):
            def take(p, t):
                dve.wait_ge(S("turned"), t + 1 + r * RUN["turned"])
                dve.sem_inc(S("xin_free"), 1)
                dve.tensor_copy(xTh[p][:, :], banks[p].bitcast(F16)[:, 0:4 * P]).then_inc(S("xth"), 1)

            def low(p, t):
                dve.wait_ge(S("hr"), t + 1 + r * RUN["hr"])
                dve.sem_inc(S("xth_free"), 1)
                dve.tensor_tensor(hq[p][:, :], hr[p][:, :], hr[p][:, :], ALU.mult).then_inc(S("hq"), 1)
                dve.wait_ge(S("hq"), t + 1 + r * RUN["hq"])
                dve.wait_ge(S("hh"), t + 1 + r * RUN["hh"])
                dve.tensor_tensor(hl[p][:, :], hq[p][:, :], hh[p][:, :], ALU.subtract).then_inc(S("hl"), 1)
                dve.wait_ge(S("hl"), t + 1 + r * RUN["hl"])
                dve.sem_inc(S("hl_free"), 1)

            take(0, 0)
            take(1, 1)
            low(0, 0)
            with dve.Fori(0, NS // 2 - 1) as i:
                take(0, i * 2 + 2)
                low(1, i * 2 + 1)
                take(1, i * 2 + 3)
                low(0, i * 2 + 2)
            low(1, NS - 1)

        def combine_pool(pool, r):
            for p in range(2):
                pool.wait_ge(S(f"yst_{p}"), 16 * (NS // 2) + r * RUN["yst"])
            pool.wait_ge(S("slots"), 1 + r * RUN["slots"])
            with pool.Fori(0, NT // 2) as i:
                for p in range(2):
                    k = i * 2 + p
                    pool.wait_ge(S("yg_free"), k + 1 + r * RUN["yg_free"])
                    hold(pool, "pool")
                    pool.tensor_copy(gi[p][:, :], row(slots, k, 2)).then_inc(S("gi"), 1)
                    pool.wait_ge(S("gi"), k + 1 + r * RUN["gi"])
                    hold(pool, "pool")
                    for j in range(2):
                        pool.indirect_dma_start(yg[p][j][:, :], None, yrows,
                                                bass.IndirectOffsetOnAxis(ap=gi[p][:, j:j + 1], axis=0))\
                            .then_inc(S(f"yg_{p}"), 16)

        def combine_dve(dve, r):
            with dve.Fori(0, NT // 2) as i:
                for p in range(2):
                    k = i * 2 + p
                    dve.wait_ge(S(f"yg_{p}"), i * 32 + 32 + r * RUN["yg"])
                    for j in range(2):
                        dve.scalar_tensor_tensor(out=Xk(k), in0=yg[p][j][:, :], scalar=wts[:, ds(k * 2 + j, 1)],
                                                 in1=Xk(k), op0=ALU.mult, op1=ALU.add).then_inc(S("xnew"), 1)
                        dve.wait_ge(S("xnew"), k * 2 + (j + 1) + r * RUN["xnew"])
                    dve.sem_inc(S("yg_free"), 1)

        def vc(i, j=0, n=None):
            return vec[:, V_OFF[i] + j:V_OFF[i] + j + (n or V_W[i])]

        def heads(ap, n):
            return ap.unsqueeze(2).to_broadcast([ap.shape[0], NH, n])

        def by_head(ap):
            return ap.rearrange("p (h e) -> p h e", h=NH)

        def taps(p, lo, n):
            return U[p][:, :].rearrange("p (j b t) -> p j b t", b=B, t=QT + DC - 1)[:, :, :, lo:lo + n]

        def mamba_load(sp):
            for t, name in ((wz, "wz"), (wx, "wx"), (wbc, "wbc"), (wdt, "wdt"), (wo, "wo")):
                sp.dma_start(t[:, :].rearrange("p (c n) -> p c n", n=a[name].shape[1]),
                             a[name].rearrange("(c p) n -> p c n", p=P)).then_inc(S("m_in"), 16)
            sp.dma_start(vec[:, :], a["vectors"]).then_inc(S("m_in"), 16)

        def pipeline(eng, turn):
            turn(-2, "A")
            turn(-1, "AB")
            turn(0, "ABC")
            turn(1, "ABCD")
            with eng.Fori(1, NT // 2 - 1) as n:
                turn(n * 2, "ABCD", 0)
                turn(n * 2 + 1, "ABCD", 1)
            turn(NT - 2, "BCD")
            turn(NT - 1, "CD")
            turn(NT, "D")

        def after(eng, name, count):
            if not isinstance(count, int) or count > 0:
                eng.wait_ge(S(name), count)

        def parity(i, odd):
            return (i if odd is None else odd) % 2

        NTAP = DC * (NB + 1)
        GRP = NH // 4 * QT

        def mamba_dve(dve):
            dve.wait_ge(S("m_in"), 16 * 6)
            dve.memset(Hs[:, :], 0.0).then_inc(S("m_state"), 1)
            dve.tensor_scalar(negA[:, :], vc(V_AL), A_LOG_MAX, None, ALU.min).then_inc(S("m_alog"), 1)
            dve.wait_ge(S("m_expA"), 1)
            dve.tensor_scalar(negA[:, :], negA[:, :], -1.0, None, ALU.mult).then_inc(S("m_negA"), 1)
            dve.wait_ge(S("m_negA"), 1)
            ca = Chain(dve, S("m_chain_a"), 8)
            cb_ = Chain(dve, S("m_chain_b"), 15)
            ce = Chain(dve, S("m_chain_e"), 3)
            cd = Chain(dve, S("m_chain_d"), 2)
            v, nab, e_, den_, s_, s2, q, l = (dv[:, n * NH:(n + 1) * NH] for n in range(8))

            def combine(k, p):
                ca.at(k)
                dve.wait_ge(S(f"yg_{p}"), k * 16 + (32 - 16 * p))
                for j in range(2):
                    ca.link(dve.scalar_tensor_tensor(out=Xk(k), in0=yg[p][j][:, :], scalar=wts[:, ds(k * 2 + j, 1)],
                                                     in1=Xk(k), op0=ALU.mult, op1=ALU.add))
                dve.sem_inc(S("yg_free"), 1)
                ca.link(dve.bn_stats(ma[:, 0:6], Xk(k)))
                hold(dve, "dve")
                ca.link(dve.bn_aggr(ma[:, 6:8], ma[:, 0:6]))
                dve.tensor_scalar(ma[:, 8:9], ma[:, 7:8], EPS, None, ALU.add).then_inc(S("m_va"), 1)

            def norm(k, p):
                dve.wait_ge(S("m_ra"), k + 1)
                ca.link(dve.tensor_scalar(xm[:, :], Xk(k), ma[:, 6:7], ma[:, 9:10], ALU.subtract, ALU.mult))
                ca.link(dve.bn_stats(mb[:, 0:6], xm[:, :]))
                hold(dve, "dve")
                ca.link(dve.bn_aggr(mb[:, 6:8], mb[:, 0:6]))
                dve.tensor_scalar(mb[:, 8:9], mb[:, 7:8], EPS, None, ALU.add).then_inc(S("m_vb"), 1)

            def norm2(k, p):
                ca.link(dve.tensor_tensor(Xk(k), Xk(k), xm[:, :], ALU.add))
                ca.done()
                dve.wait_ge(S("m_rb"), k + 1)
                dve.tensor_scalar(xn[:, :], xm[:, :], mb[:, 6:7], mb[:, 9:10], ALU.subtract, ALU.mult)\
                    .then_inc(S("m_xn"), 1)

            def dt_in(k, p):
                dve.wait_ge(S("m_dtp"), k + 1)
                dve.tensor_tensor(v, banks[0][:, 2 * P:2 * P + NH], vc(V_DTB), ALU.add).then_inc(S("m_v"), 1)
                dve.wait_ge(S("m_v"), k + 1)
                dve.scalar_tensor_tensor(out=nab, in0=v, scalar=-1.0, in1=v, op0=ALU.mult, op1=ALU.min)\
                    .then_inc(S("m_nab"), 1)

            def dt_out(k, p):
                cb_.at(k)
                dve.wait_ge(S("m_e"), k + 1)
                cb_.link(dve.tensor_scalar(den_, e_, 2.0, None, ALU.add))
                cb_.link(dve.reciprocal(den_, den_))
                cb_.link(dve.tensor_tensor(s_, e_, den_, ALU.mult))
                cb_.link(dve.tensor_tensor(s2, s_, s_, ALU.mult))
                cb_.link(dve.tensor_scalar(q, s2, 1.0 / 15, None, ALU.mult))
                for c in (13, 11, 9, 7, 5, 3):
                    cb_.link(dve.scalar_tensor_tensor(out=q, in0=q, scalar=1.0 / c, in1=s2, op0=ALU.add, op1=ALU.mult))
                cb_.link(dve.scalar_tensor_tensor(out=l, in0=q, scalar=1.0, in1=s_, op0=ALU.add, op1=ALU.mult))
                cb_.link(dve.tensor_scalar(v, v, 0.0, None, ALU.max))
                cb_.link(dve.scalar_tensor_tensor(out=dt_[p][:, :], in0=l, scalar=2.0, in1=v, op0=ALU.mult, op1=ALU.add))
                cb_.link(dve.scalar_tensor_tensor(out=a_[p][:, :], in0=dt_[p][:, :], scalar=DOWN, in1=negA[:, :],
                                                  op0=ALU.mult, op1=ALU.mult))
                dve.tensor_scalar(a_[p][:, :], a_[p][:, :], CLAMP * DOWN, 1.0 / DOWN, ALU.max, ALU.mult)\
                    .then_inc(S("m_a"), 1)
                cb_.done()

            def conv(k, p):
                dve.wait_ge(S("m_U"), k + 1)
                dve.wait_ge(S("m_hist"), k + 1)
                for c in range(DC):
                    for j in range(NB + 1):
                        o = cv[:, j * P:(j + 1) * P].rearrange("p (b t) -> p b t", t=QT)
                        u = taps(p, c, QT)[:, j]
                        if c == 0:
                            m = dve.tensor_scalar(o, u, vc(V_CW, j * DC, 1), vc(V_CB, j, 1), ALU.mult, ALU.add)
                        else:
                            dve.wait_ge(S("m_tap"), k * NTAP + ((c - 1) * (NB + 1) + j + 1))
                            m = dve.scalar_tensor_tensor(out=o, in0=u, scalar=vc(V_CW, j * DC + c, 1), in1=o,
                                                         op0=ALU.mult, op1=ALU.add)
                        m.then_inc(S("m_tap"), 1)

            def silu(k, p):
                dve.wait_ge(S("m_th"), k + 1)
                ce.at(k)
                ce.link(dve.scalar_tensor_tensor(out=th[:, :], in0=th[:, :], scalar=1.0, in1=cv[:, :],
                                                  op0=ALU.add, op1=ALU.mult))
                n = B * DS_
                dve.tensor_tensor(bm[:, :], th[0:n, NB * P:], const(C_HALF)[0:n, :], ALU.mult).then_inc(S("m_g"), 1)
                dve.tensor_tensor(cm[p][:, :], th[n:2 * n, NB * P:], const(C_HALF)[n:2 * n, :], ALU.mult)\
                    .then_inc(S("m_g"), 1)

            def cbs(k, p):
                dve.wait_ge(S("m_cbp"), k + 1)
                dve.tensor_copy(bt[p][:, :], banks[2][:, 0:B * DS_])
                ce.link(dve.tensor_reduce(cbr[:, :], banks[2][:, P:2 * P].rearrange("p (b t) -> p t b", b=B), AX.X, ALU.add))
                dve.tensor_tensor(cb[p][:, :], cbr[:, :], const(C_QM), ALU.mult).then_inc(S("m_cb"), 1)
                dve.wait_ge(S("m_xs"), k + 1)
                ce.link(dve.tensor_tensor(by_head(dtx[p][:, :]), by_head(xs[p][:, :]), heads(dt_[p][:, :], HP), ALU.mult))
                dve.sem_inc(S("m_dtx"), 1)
                ce.done()

            def gate_in(k, p):
                dve.wait_ge(S("m_tz"), k + 1)
                dve.scalar_tensor_tensor(out=gz[p][:, :], in0=tz[:, :], scalar=1.0, in1=banks[3][:, :],
                                         op0=ALU.add, op1=ALU.mult).then_inc(S("m_gz"), 1)

            def carried(k, p):
                dve.wait_ge(S("m_ee"), k + 1)
                dve.tensor_tensor(by_head(dtxw[:, :]), by_head(dtx[p][:, :]), heads(ee[:, NH:2 * NH], HP), ALU.mult)\
                    .then_inc(S("m_dtxw"), 1)
                dve.wait_ge(S("m_inter"), k + 1)
                dve.tensor_tensor(by_head(yi[p][:, :]), by_head(banks[7][:, :]), heads(ee[:, 0:NH], HP), ALU.mult)\
                    .then_inc(S("m_yi"), 1)

            def state(k, p):
                dve.wait_ge(S("m_sp"), k + 1)
                dve.wait_ge(S("m_Hd"), k + 1)
                dve.tensor_tensor(Hs[:, :], Hs[:, :], banks[7][0:B * DS_, :], ALU.add).then_inc(S("m_state"), 1)

            def decays(k, p, lo):
                for g in (lo, lo + 1):
                    dve.wait_ge(S("m_L"), k * 4 + (g + 1))
                    u = R[p][:, g * GRP:(g + 1) * GRP].rearrange("p (h t) -> p h t", t=QT)
                    dve.tensor_tensor(u, u, cb[p][:, :].unsqueeze(1).to_broadcast([P, NH // 4, QT]), ALU.mult)\
                        .then_inc(S("m_M"), 1)

            def gate(k, p):
                cd.at(k)
                dve.wait_ge(S("m_t1"), k + 1)
                cd.link(dve.tensor_tensor(yi[p][:, :], yi[p][:, :], xd[:, :], ALU.add))
                dve.tensor_tensor(G[:, :], yi[p][:, :], gz[p][:, :], ALU.mult).then_inc(S("m_G"), 1)

            def finish(k, p):
                dve.wait_ge(S("m_o"), k + 1)
                dve.wait_ge(S("m_rr"), k + 1)
                cd.link(dve.scalar_tensor_tensor(out=Xk(k), in0=banks[5][:, 0:D], scalar=mss[:, 2:3], in1=Xk(k),
                                                 op0=ALU.mult, op1=ALU.add))
                dve.sem_inc(S("m_x"), 1)
                cd.done()

            def turn(i, parts, odd=None):
                p = parity(i, odd)
                if "C" in parts:
                    carried(i, p)
                if "A" in parts:
                    combine(i + 2, p)
                if "C" in parts:
                    decays(i, p, 0)
                if "D" in parts:
                    gate(i - 1, 1 - p)
                if "C" in parts:
                    state(i, p)
                if "A" in parts:
                    norm(i + 2, p)
                if "C" in parts:
                    decays(i, p, 2)
                if "A" in parts:
                    norm2(i + 2, p)
                if "B" in parts:
                    conv(i + 1, 1 - p)
                if "C" in parts:
                    gate_in(i, p)
                if "D" in parts:
                    finish(i - 1, 1 - p)
                if "A" in parts:
                    dt_in(i + 2, p)
                if "B" in parts:
                    silu(i + 1, 1 - p)
                if "A" in parts:
                    dt_out(i + 2, p)
                if "B" in parts:
                    cbs(i + 1, 1 - p)

            pipeline(dve, turn)

        def mamba_pool(pool):
            pool.wait_ge(S("m_in"), 16 * 6)
            pool.wait_ge(S("slots"), 1)
            for p in range(2):
                pool.wait_ge(S(f"yst_{p}"), 16 * (NS // 2))
            pool.memset(taps(1, QT, DC - 1), 0.0).then_inc(S("m_hist_set"), 1)
            pool.sem_inc(S("yg_free"), 2)

            def gather(k, p):
                pool.wait_ge(S("yg_free"), k + 1)
                hold(pool, "pool")
                pool.tensor_copy(gi[p][:, :], row(slots, k, 2)).then_inc(S("gi"), 1)
                pool.wait_ge(S("gi"), k + 1)
                hold(pool, "pool")
                for j in range(2):
                    pool.indirect_dma_start(yg[p][j][:, :], None, yrows,
                                            bass.IndirectOffsetOnAxis(ap=gi[p][:, j:j + 1], axis=0))\
                        .then_inc(S(f"yg_{p}"), 16)

            def power(sem_in, sem_out, ap_in, ap_out, k):
                pool.wait_ge(S(sem_in), k + 1)
                hold(pool, "pool")
                pool.tensor_tensor(ap_out, ap_in, mhalf[:, 0:1], ALU.pow).then_inc(S(sem_out), 1)

            def history(k, p):
                pool.wait_ge(S("m_U"), k) if not isinstance(k, int) or k else pool.wait_ge(S("m_hist_set"), 1)
                after(pool, "m_tap", (k - 1) * NTAP)
                hold(pool, "pool")
                for j in range(NB + 1):
                    m = pool.tensor_copy(taps(p, 0, DC - 1)[:, j], taps(1 - p, QT, DC - 1)[:, j])
                m.then_inc(S("m_hist"), 1)

            def exponents(k, p):
                pool.wait_ge(S("m_a"), k + 1)
                after(pool, "m_intra", (k - 1) * 2)
                hold(pool, "pool")
                for g in range(4):
                    n = NH // 8
                    pairs = a_[p][:, (g // 2) * (NH // 2):(g // 2 + 1) * (NH // 2)].rearrange("p (x r) -> p r x", x=2)
                    pool.tensor_tensor(R[p][:, g * GRP:(g + 1) * GRP].rearrange("p (r x t) -> p r x t", x=2, t=QT),
                                       pairs[:, g % 2 * n:(g % 2 + 1) * n].unsqueeze(3).to_broadcast([P, n, 2, QT]),
                                       const(C_QM).unsqueeze(1).unsqueeze(1).to_broadcast([P, n, 2, QT]), ALU.mult)\
                        .then_inc(S("m_R"), 1)

            def state(k, p):
                pool.wait_ge(S("m_yi"), k + 1)
                hold(pool, "pool")
                pool.tensor_tensor(by_head(Hs[:, :]), by_head(Hs[:, :]), heads(dd[:, :], HP), ALU.mult)\
                    .then_inc(S("m_Hd"), 1)

            def skip_path(k, p):
                after(pool, "m_G", k)
                hold(pool, "pool")
                pool.tensor_tensor(by_head(xd[:, :]), by_head(xs[p][:, :]), heads(vc(V_DP), HP), ALU.mult)\
                    .then_inc(S("m_xd"), 1)

            def add_moved(k, p):
                pool.wait_ge(S("m_xd"), k + 1)
                pool.wait_ge(S("m_y2"), k * (16 * NMOVE) + 16 * NMOVE)
                hold(pool, "pool")
                pool.tensor_tensor(xd[:, :], xd[:, :], y2[:, :], ALU.add).then_inc(S("m_t1"), 1)

            def rms(k, p):
                pool.wait_ge(S("m_ss"), k + 1)
                hold(pool, "pool")
                pool.tensor_scalar(mss[:, 1:2], mss[:, 0:1], 1.0 / DI, 4.0 * EPS, ALU.mult, ALU.add)\
                    .then_inc(S("m_ms"), 1)
                power("m_ms", "m_rr", mss[:, 1:2], mss[:, 2:3], k)

            def turn(i, parts, odd=None):
                p = parity(i, odd)
                if "A" in parts:
                    gather(i + 2, p)
                    history(i + 2, p)
                if "D" in parts:
                    skip_path(i - 1, 1 - p)
                if "C" in parts:
                    state(i, p)
                if "A" in parts:
                    power("m_va", "m_ra", ma[:, 8:9], ma[:, 9:10], i + 2)
                if "D" in parts:
                    add_moved(i - 1, 1 - p)
                if "A" in parts:
                    power("m_vb", "m_rb", mb[:, 8:9], mb[:, 9:10], i + 2)
                if "D" in parts:
                    rms(i - 1, 1 - p)
                if "B" in parts:
                    exponents(i + 1, 1 - p)

            pipeline(pool, turn)

        NMOVE = B * 4

        def mamba_sync(sp):
            def move(k):
                after(sp, "m_t1", k)
                for j in range(4):
                    if j % 2 == 0:
                        sp.wait_ge(S("m_y1"), k * 2 + (j // 2 + 1))
                    for b in range(B):
                        sp.dma_start(y2[b * QT:(b + 1) * QT, j * P:(j + 1) * P], y1[j * QT:(j + 1) * QT, b * P:(b + 1) * P])\
                            .then_inc(S("m_y2"), 16)
            move(0)
            with sp.Fori(1, NT) as k:
                move(k)

        def mamba_act(act):
            act.wait_ge(S("m_in"), 16 * 6)
            act.wait_ge(S("m_alog"), 1)
            act.activation(negA[:, :], negA[:, :], ACT.Exp).then_inc(S("m_expA"), 1)

            def normed(k, p):
                act.wait_ge(S("m_xT"), k + 1)
                for c in range(KD):
                    m = act.activation(xnT[p][:, c * P:(c + 1) * P], banks[0][:, c * P:(c + 1) * P], ACT.Identity,
                                       scale=vc(V_LNW, c, 1), bias=vc(V_LNB, c, 1))
                m.then_inc(S("m_xnT"), 1)

            def channels(k, p):
                act.wait_ge(S("m_up"), k + 1)
                act.activation(taps(p, DC - 1, QT)[:, 0:NB], banks[1][:, :].rearrange("p (j b t) -> p j b t", b=B, t=QT),
                               ACT.Copy).then_inc(S("m_U1"), 1)
                act.activation(taps(p, DC - 1, QT)[:, NB], banks[2][:, 0:P].rearrange("p (b t) -> p b t", t=QT),
                               ACT.Copy).then_inc(S("m_U"), 1)

            def out_of_heads(k, p, g):
                after(act, "m_y2", k * (16 * NMOVE))
                act.wait_ge(S("m_intra"), k * 2 + (g + 1))
                for n in range(2):
                    for x in range(2):
                        j = 2 * g + x
                        o = y1[j * QT:(j + 1) * QT, :].rearrange("t (b r e) -> t r b e", b=B, e=HP)
                        u = banks[6 + n][j * QT:(j + 1) * QT, :].rearrange("t (r x b e) -> t r x b e", x=2, b=B, e=HP)
                        m = act.activation(o[:, n * 8:(n + 1) * 8], u[:, :, x], ACT.Copy)
                m.then_inc(S("m_y1"), 1)

            def turn(i, parts, odd=None):
                p = parity(i, odd)
                if "C" in parts:
                    act.wait_ge(S("m_ep"), i + 1)
                    act.activation(ee[:, :], banks[0][:, 0:2 * NH], ACT.Exp)
                    act.activation(dd[:, :], banks[0][0:B * DS_, 2 * NH:3 * NH], ACT.Exp).then_inc(S("m_ee"), 1)
                    for g in range(4):
                        act.wait_ge(S("m_Lp"), i * 4 + (g + 1))
                        act.activation(R[p][:, g * GRP:(g + 1) * GRP], banks[4 + g % 2][:, :], ACT.Exp).then_inc(S("m_L"), 1)
                        if g == 1:
                            act.wait_ge(S("m_dtx"), i + 1)
                            after(act, "m_intra", i * 2)
                            for b in range(B):
                                m = act.activation(bd.rearrange("p (h b e) -> p h b e", b=B, e=HP)[:, :, b, :],
                                                   by_head(dtx[p][:, :]), ACT.Copy, scale=const(C_BM)[:, b:b + 1])
                            m.then_inc(S("m_bd"), 1)
                if "D" in parts:
                    act.wait_ge(S("m_G"), i)
                    act.activation(tz[:, :], G[:, :], ACT.Square, accum_out=mss[:, 0:1]).then_inc(S("m_ss"), 1)
                    act.wait_ge(S("m_GTp"), i)
                    for j in range(NB):
                        m = act.activation(GT[:, j * P:(j + 1) * P], banks[1][:, j * P:(j + 1) * P], ACT.Copy,
                                           scale=vc(V_RMS, j, 1))
                    m.then_inc(S("m_GT"), 1)
                if "C" in parts:
                    act.wait_ge(S("m_z"), i + 1)
                    after(act, "m_ss", i)
                    act.activation(tz[:, :], banks[3][:, :], ACT.Tanh, scale=0.5).then_inc(S("m_tz"), 1)
                if "A" in parts:
                    normed(i + 2, p)
                if "C" in parts:
                    out_of_heads(i, p, 0)
                if "A" in parts:
                    channels(i + 2, p)
                if "B" in parts:
                    act.wait_ge(S("m_tap"), (i + 2) * NTAP)
                    act.activation(th[:, :], cv[:, :], ACT.Tanh, scale=0.5).then_inc(S("m_th"), 1)
                if "A" in parts:
                    act.wait_ge(S("m_nab"), i + 3)
                    act.activation(dv[:, 2 * NH:3 * NH], dv[:, NH:2 * NH], ACT.Exp).then_inc(S("m_e"), 1)
                if "C" in parts:
                    out_of_heads(i, p, 1)
                if "B" in parts:
                    act.wait_ge(S("m_xsp"), i + 2)
                    after(act, "m_xd", i)
                    act.activation(xs[1 - p][:, :], banks[4][:, :], ACT.Copy, scale=0.5).then_inc(S("m_xs"), 1)

            pipeline(act, turn)

        def mamba_pe(pe):
            pe.wait_ge(S("m_in"), 16 * 6)

            def proj(o, w, n, lo, xp, tokens_first):
                for c in range(KD):
                    x = xnT[xp][:, c * P:(c + 1) * P]
                    ww = w[:, c * n + lo:c * n + lo + (n if tokens_first else P)]
                    m = pe.matmul(o, x if tokens_first else ww, ww if tokens_first else x, start=c == 0, stop=c == KD - 1)
                return m

            def gate_in(k, p):
                after(pe, "m_gz", k)
                proj(banks[3][:, :], wz, DI, 0, p, True).then_inc(S("m_z"), 1)

            def sums(k, p):
                pe.wait_ge(S("m_a"), k + 1)
                if not (isinstance(k, int) and k == NT - 1):
                    pe.wait_ge(S("m_v"), k + 2)
                pe.matmul(banks[0][:, 0:NH], const(C_INC), a_[p][:, :], start=True, stop=True)
                pe.matmul(banks[0][:, NH:2 * NH], const(C_GT), a_[p][:, :], start=True, stop=True)
                pe.matmul(banks[0][0:B * DS_, 2 * NH:3 * NH], const(C_BLK), a_[p][:, :], start=True, stop=True)\
                    .then_inc(S("m_ep"), 1)

            def inter(k, p):
                pe.wait_ge(S("m_state"), k + 1)
                after(pe, "m_y1", k * 2)
                pe.matmul(banks[7][:, :], cm[p][:, :], Hs[:, :], start=True, stop=True).then_inc(S("m_inter"), 1)

            def decays(k, p, gs):
                for g in gs:
                    pe.wait_ge(S("m_R"), k * 4 + (g + 1))
                    if g >= 2:
                        pe.wait_ge(S("m_L"), k * 4 + (g - 1))
                    elif g == 0:
                        pe.wait_ge(S("m_xs"), k + 1)
                    else:
                        after(pe, "m_x", k - 1)
                    pe.matmul(banks[4 + g % 2][:, :], const(C_GT), R[p][:, g * GRP:(g + 1) * GRP], start=True, stop=True)\
                        .then_inc(S("m_Lp"), 1)

            def state(k, p):
                pe.wait_ge(S("m_yi"), k + 1)
                pe.wait_ge(S("m_dtxw"), k + 1)
                pe.matmul(banks[7][0:B * DS_, :], bt[p][:, :], dtxw[:, :], start=True, stop=True).then_inc(S("m_sp"), 1)

            def intra(k, p, g):
                if g == 0:
                    pe.wait_ge(S("m_bd"), k + 1)
                    pe.wait_ge(S("m_state"), k + 2)
                    after(pe, "m_y1", k * 2)
                pe.wait_ge(S("m_M"), k * 4 + (2 * g + 2))
                mv_ = R[p].rearrange("p (g r c) -> p g r c", g=2, c=2 * QT)
                bv = bd.rearrange("p (g x r c) -> p g r x c", g=2, x=2, c=B * HP)
                for r in range(NH // 4):
                    n, c = r // 8, r % 8
                    m = pe.matmul(banks[6 + n][2 * g * QT:2 * (g + 1) * QT, c * 64:(c + 1) * 64], mv_[:, g, r], bv[:, g, r],
                                  start=True, stop=True)
                m.then_inc(S("m_intra"), 1)

            def turned_gate(k, p):
                pe.wait_ge(S("m_G"), k + 1)
                if not (isinstance(k, int) and k >= NT - 2):
                    pe.wait_ge(S("m_U1"), k + 3)
                for j in range(NB):
                    m = pe.transpose(banks[1][:, j * P:(j + 1) * P], G[:, j * P:(j + 1) * P], ident)
                m.then_inc(S("m_GTp"), 1)

            def project_out(k, p):
                pe.wait_ge(S("m_GT"), k + 1)
                if not (isinstance(k, int) and k == NT - 1):
                    pe.wait_ge(S("m_L"), k * 4 + 8)
                for j in range(NB):
                    m = pe.matmul(banks[5][:, 0:D], GT[:, j * P:(j + 1) * P], wo[:, j * D:(j + 1) * D],
                                  start=j == 0, stop=j == NB - 1)
                m.then_inc(S("m_o"), 1)

            def turned_norm(k, p):
                pe.wait_ge(S("m_xn"), k + 1)
                after(pe, "m_ee", k - 1)
                for c in range(KD):
                    m = pe.transpose(banks[0][:, c * P:(c + 1) * P], xn[:, c * P:(c + 1) * P], ident)
                m.then_inc(S("m_xT"), 1)

            def project_in(k, p):
                pe.wait_ge(S("m_xnT"), k + 1)
                proj(banks[0][:, 2 * P:2 * P + NH], wdt, NH, 0, p, True).then_inc(S("m_dtp"), 1)
                after(pe, "m_cb", k - 1)
                proj(banks[2][:, 0:P], wbc, P, 0, p, False)
                after(pe, "m_GT", k - 3)
                for j in range(NB):
                    m = proj(banks[1][:, j * P:(j + 1) * P], wx, DI, j * P, p, False)
                m.then_inc(S("m_up"), 1)

            def turned_channels(k, p):
                pe.wait_ge(S("m_g"), k * 2 + 2)
                after(pe, "m_L", k * 4)
                for j in range(NB):
                    m = pe.transpose(banks[4][:, j * P:(j + 1) * P], th[:, j * P:(j + 1) * P], ident)
                m.then_inc(S("m_xsp"), 1)
                n = B * DS_
                if not (isinstance(k, int) and k == NT - 1):
                    pe.wait_ge(S("m_U"), k + 2)
                pe.matmul(banks[2][:, P:2 * P], bm[:, :], cm[p][:, :], start=True, stop=True)
                pe.transpose(banks[2][:, 0:n], bm[:, :], ident[0:n, 0:n]).then_inc(S("m_cbp"), 1)

            def turn(i, parts, odd=None):
                p = parity(i, odd)
                if "C" in parts:
                    sums(i, p)
                    inter(i, p)
                    decays(i, p, (0, 1))
                    state(i, p)
                    decays(i, p, (2, 3))
                if "D" in parts:
                    turned_gate(i - 1, 1 - p)
                if "C" in parts:
                    gate_in(i, p)
                if "D" in parts:
                    project_out(i - 1, 1 - p)
                if "A" in parts:
                    turned_norm(i + 2, p)
                if "C" in parts:
                    intra(i, p, 0)
                if "A" in parts:
                    project_in(i + 2, p)
                if "C" in parts:
                    intra(i, p, 1)
                if "B" in parts:
                    turned_channels(i + 1, 1 - p)

            pipeline(pe, turn)

        def store_out(sp, r):
            for g in range(4):
                n = NT // 4
                sp.wait_ge(S("xnew"), 2 * n * (g + 1))
                for b in range(B):
                    sp.dma_start(out[b].rearrange("(k t) d -> t k d", t=QT)[:, g * n:(g + 1) * n, :],
                                 X[b * QT:(b + 1) * QT, g * n * D:(g + 1) * n * D].rearrange("t (k d) -> t k d", d=D))\
                        .then_inc(S("stored"), 16)
            sp.wait_ge(S("stored"), 16 * B * 4)

        block = ctx.enter_context(nc.Block())

        @block.sync
        def _(sp):
            sync_load(sp)
            mamba_load(sp)
            experts_sync(sp, 0)
            mamba_sync(sp)
            experts_sync(sp, 1)
            store_out(sp, 1)

        @block.scalar
        def _(act):
            split_weights(None, act)
            route_act(act, 0)
            experts_act(act, 0)
            mamba_act(act)
            route_act(act, 1)
            experts_act(act, 1)

        @block.gpsimd
        def _(pool):
            pool_rstd(pool, 0)
            route_pool(pool, 0)
            experts_store(pool, 0)
            mamba_pool(pool)
            pool_rstd(pool, 1)
            route_pool(pool, 1)
            experts_store(pool, 1)
            combine_pool(pool, 1)

        @block.vector
        def _(dve):
            dve.wait_ge(S("x_in"), 16 * B)
            stats(dve, 0)
            split_weights(dve, None)
            route_dve(dve, 0)
            experts_dve(dve, 0)
            mamba_dve(dve)
            stats(dve, 1)
            route_dve(dve, 1)
            experts_dve(dve, 1)
            combine_dve(dve, 1)

        @block.tensor
        def _(pe):
            route_pe(pe, 0)
            experts_pe(pe, 0)
            mamba_pe(pe)
            route_pe(pe, 1)
            experts_pe(pe, 1)


def constants():
    import numpy as np
    p = np.arange(P)[:, None]
    q = np.arange(P)[None, :]
    same = p // QT == q // QT
    parts = {
        C_ID: p == q,
        C_INC: same & (p <= q),
        C_GT: same & (p > q),
        C_BLK: p // QT == (np.arange(B * DS_)[None, :] // DS_),
        C_HALF: 0.5 * (p % (B * DS_) // DS_ == q // QT),
        C_QM: p % QT <= np.arange(QT)[None, :],
        C_BM: p // QT == np.arange(B)[None, :],
        C_IOTA: np.broadcast_to(np.arange(E)[None, :], (P, E)),
        C_ECAP: np.broadcast_to(CAP * np.arange(E)[None, :], (P, E)),
        C_TRI: p,
        C_TAB: np.broadcast_to(np.arange(NS)[None, :], (P, NS)),
    }
    c32 = np.concatenate([np.asarray(parts[i], np.float32) for i in range(len(C_W))], axis=1)
    c16 = np.concatenate([p == q, p < q, np.ones((P, P), bool)], axis=1).astype(np.float16)
    return np.ascontiguousarray(c32), c16


def kernel(**inputs):
    import numpy as np
    import concourse.bacc as bacc
    from concourse.bass_utils import run_bass_kernel_spmd

    g = {k.replace("L0_", ""): np.asarray(v) for k, v in inputs.items()}
    c32, c16 = constants()
    W = g["attn_W_in"]
    channels = np.concatenate([np.arange(DI), DI + np.arange(2 * DS_).reshape(2, 1, DS_).repeat(B, 1).ravel()])
    cw = g["attn_conv_w"][:, 0, channels].reshape(DC, NB + 1, P).transpose(2, 1, 0).reshape(P, -1)
    cbias = g["attn_conv_b"][channels].reshape(NB + 1, P).T
    rows = [np.broadcast_to(g[n], (P, NH)) for n in ("attn_dt_bias", "attn_Dp", "attn_A_log")]
    vectors = np.concatenate([g["attn_ln_w"].reshape(KD, P).T, g["attn_ln_b"].reshape(KD, P).T, cw, cbias,
                              g["attn_rms_w"].reshape(NB, P).T] + rows, axis=1)
    arrays = {
        "x": g["attn_x"], "router": g["ffn_router_w"].T, "w1": g["ffn_w1"], "w2": g["ffn_w2"],
        "wz": W[:, 0:DI], "wx": W[:, DI:2 * DI],
        "wbc": W[:, 2 * DI:][:, np.arange(2 * DS_).reshape(2, 1, DS_).repeat(B, 1).ravel()],
        "wdt": W[:, -NH:], "wo": g["attn_W_out"], "vectors": vectors,
        "consts": c32, "consts16": c16,
    }
    arrays = {k: np.ascontiguousarray(v) for k, v in arrays.items()}
    nc = bacc.Bacc("TRN2", target_bir_lowering=False, num_devices=1)
    a = {k: nc.dram_tensor(f"in_{k}", v.shape, mybir.dt.from_np(v.dtype), kind="ExternalInput").ap()
         for k, v in arrays.items()}
    out = nc.dram_tensor("out", (B, T, D), F32, kind="ExternalOutput").ap()
    build(nc, a, out)
    r = run_bass_kernel_spmd(nc, [{f"in_{k}": v for k, v in arrays.items()}], core_ids=[0])
    return r.results[0]["out"]
```
